# Optimizing a Trainium2 kernel written in Bass

```python
import numpy as np
import jax
import jax.numpy as jnp

def _softmax(x, axis=-1):
    return jax.nn.softmax(x, axis=axis)

def _gelu(x):
    return jax.nn.gelu(x, approximate=True)

def _silu(x):
    return jax.nn.silu(x)

def _sigmoid(x):
    return jax.nn.sigmoid(x)

def _layernorm(x, axis=-1, eps=1e-05):
    m = jnp.mean(x, axis=axis, keepdims=True)
    v = jnp.var(x, axis=axis, keepdims=True)
    return (x - m) / jnp.sqrt(v + eps)

def _scatter_add(tgt, idx, src, axis=0):
    return tgt.at[idx].add(src)

def _segment_sum(src, seg, n):
    return jax.ops.segment_sum(src, seg, n)
kernel_name = 'mk_seq_postln_d1_jaxref_r4_d14bf5'

def setup_inputs(seed: int=0):
    np.random.seed(seed)
    _w = jnp.asarray

    def _L0_attn_setup():
        import jax, jax.numpy as jnp
        import numpy as np
        B, L, D = (2, 512, 256)
        H = 16
        DH = D // H
        FACTOR = 0.6
        U = max(1, min(L, int(FACTOR * L)))

        def _split_heads(x):
            b, l, d = x.shape
            return x.reshape(b, l, H, DH).transpose(0, 2, 1, 3)
        key = jax.random.key(seed)
        ks = jax.random.split(key, 9)
        s = 0.02
        return {'x': jax.random.normal(ks[0], (B, L, D), dtype=jnp.float32), 'Wq': jax.random.normal(ks[1], (D, D), dtype=jnp.float32) * s, 'bq': jnp.zeros((D,), dtype=jnp.float32), 'Wk': jax.random.normal(ks[2], (D, D), dtype=jnp.float32) * s, 'bk': jnp.zeros((D,), dtype=jnp.float32), 'Wv': jax.random.normal(ks[3], (D, D), dtype=jnp.float32) * s, 'bv': jnp.zeros((D,), dtype=jnp.float32), 'Wo': jax.random.normal(ks[4], (D, D), dtype=jnp.float32) * s, 'bo': jnp.zeros((D,), dtype=jnp.float32)}
    _L0_attn_in = _L0_attn_setup()

    def _L0_ffn_setup():
        import jax, jax.numpy as jnp
        import numpy as np
        DIM = 256

        def _reference_tuple_inner(x, W_r, W_k, W_v, mu_r, mu_k):
            B, T, C = x.shape
            x_prev = jnp.concatenate([jnp.zeros((B, 1, C), x.dtype), x[:, :-1, :]], axis=1)
            xr = mu_r * x + (1.0 - mu_r) * x_prev
            xk = mu_k * x + (1.0 - mu_k) * x_prev
            r = jax.nn.sigmoid(jnp.einsum('btc,dc->btd', xr, W_r))
            k = jnp.einsum('btc,dc->btd', xk, W_k)
            k_act = jnp.square(jax.nn.relu(k))
            out = r * jnp.einsum('btc,dc->btd', k_act, W_v)
            new_state = x[:, -1, :]
            return (out, new_state)
        key = jax.random.key(seed)
        ks = jax.random.split(key, 6)
        B, T, C = (8, 512, DIM)
        x = jax.random.normal(ks[0], (B, T, C), dtype=jnp.float32)
        s = 1.0 / np.sqrt(C)
        W_r = jax.random.uniform(ks[1], (C, C), jnp.float32, -s, s)
        W_k = jax.random.uniform(ks[2], (C, C), jnp.float32, -s, s)
        W_v = jax.random.uniform(ks[3], (C, C), jnp.float32, -s, s)
        mu_r = jax.random.uniform(ks[4], (C,), jnp.float32)
        mu_k = jax.random.uniform(ks[5], (C,), jnp.float32)
        return {'x': x, 'W_r': W_r, 'W_k': W_k, 'W_v': W_v, 'mu_r': mu_r, 'mu_k': mu_k}
    _L0_ffn_in = _L0_ffn_setup()
    _d = {'L0_attn_x': _L0_attn_in['x'], 'L0_attn_Wq': _L0_attn_in['Wq'], 'L0_attn_bq': _L0_attn_in['bq'], 'L0_attn_Wk': _L0_attn_in['Wk'], 'L0_attn_bk': _L0_attn_in['bk'], 'L0_attn_Wv': _L0_attn_in['Wv'], 'L0_attn_bv': _L0_attn_in['bv'], 'L0_attn_Wo': _L0_attn_in['Wo'], 'L0_attn_bo': _L0_attn_in['bo'], 'L0_ffn_W_r': _L0_ffn_in['W_r'], 'L0_ffn_W_k': _L0_ffn_in['W_k'], 'L0_ffn_W_v': _L0_ffn_in['W_v'], 'L0_ffn_mu_r': _L0_ffn_in['mu_r'], 'L0_ffn_mu_k': _L0_ffn_in['mu_k']}
    _x0 = _d['L0_attn_x']
    _d['L0_attn_x'] = jax.random.normal(jax.random.fold_in(jax.random.key(seed), 1), (2, 4096, 256), dtype=_x0.dtype)
    del _x0
    return _d

def reference(L0_attn_x, L0_attn_Wq, L0_attn_bq, L0_attn_Wk, L0_attn_bk, L0_attn_Wv, L0_attn_bv, L0_attn_Wo, L0_attn_bo, L0_ffn_W_r, L0_ffn_W_k, L0_ffn_W_v, L0_ffn_mu_r, L0_ffn_mu_k):

    def _L0_attn_ref(x, Wq, bq, Wk, bk, Wv, bv, Wo, bo):
        import jax, jax.numpy as jnp
        import numpy as np
        B, L, D = (2, 512, 256)
        H = 16
        DH = D // H
        FACTOR = 0.6
        U = max(1, min(L, int(FACTOR * L)))

        def _split_heads(x):
            b, l, d = x.shape
            return x.reshape(b, l, H, DH).transpose(0, 2, 1, 3)
        b, l, _ = x.shape
        scale = 1.0 / jnp.sqrt(jnp.asarray(DH, dtype=x.dtype))
        q = _split_heads(x @ Wq + bq)
        k = _split_heads(x @ Wk + bk)
        v = _split_heads(x @ Wv + bv)
        scores = jnp.einsum('bhqd,bhkd->bhqk', q, k) * scale
        sparsity = scores.max(axis=-1) - scores.mean(axis=-1)
        _, top_idx = jax.lax.top_k(sparsity, U)
        q_sel = jnp.take_along_axis(q, top_idx[..., None], axis=2)
        scores_sel = jnp.einsum('bhud,bhkd->bhuk', q_sel, k) * scale
        attn = jax.nn.softmax(scores_sel, axis=-1)
        out_sel = jnp.einsum('bhuk,bhkd->bhud', attn, v)
        bi = jnp.arange(b)[:, None, None]
        hi = jnp.arange(H)[None, :, None]
        out = jnp.zeros_like(q).at[bi, hi, top_idx].set(out_sel)
        out = out.transpose(0, 2, 1, 3).reshape(b, l, D)
        return out @ Wo + bo

    def _L0_ffn_ref(x, W_r, W_k, W_v, mu_r, mu_k):
        import jax, jax.numpy as jnp
        import numpy as np
        DIM = 256

        def _reference_tuple_inner(x, W_r, W_k, W_v, mu_r, mu_k):
            B, T, C = x.shape
            x_prev = jnp.concatenate([jnp.zeros((B, 1, C), x.dtype), x[:, :-1, :]], axis=1)
            xr = mu_r * x + (1.0 - mu_r) * x_prev
            xk = mu_k * x + (1.0 - mu_k) * x_prev
            r = jax.nn.sigmoid(jnp.einsum('btc,dc->btd', xr, W_r))
            k = jnp.einsum('btc,dc->btd', xk, W_k)
            k_act = jnp.square(jax.nn.relu(k))
            out = r * jnp.einsum('btc,dc->btd', k_act, W_v)
            new_state = x[:, -1, :]
            return (out, new_state)
        return _reference_tuple_inner(x, W_r, W_k, W_v, mu_r, mu_k)[0]
    x = L0_attn_x
    x = _layernorm(x + _L0_attn_ref(x, L0_attn_Wq, L0_attn_bq, L0_attn_Wk, L0_attn_bk, L0_attn_Wv, L0_attn_bv, L0_attn_Wo, L0_attn_bo), axis=-1)
    x = _layernorm(x + _L0_ffn_ref(x, L0_ffn_W_r, L0_ffn_W_k, L0_ffn_W_v, L0_ffn_mu_r, L0_ffn_mu_k), axis=-1)
    return x

_drawn_inputs = setup_inputs


def setup_inputs(seed=0):
    import zlib

    import numpy as np

    out = dict(_drawn_inputs(seed))
    spreads = {'L0_attn_bq': (0.0, 0.8),
     'L0_attn_bk': (0.0, 0.8),
     'L0_attn_bv': (0.0, 0.8),
     'L0_attn_bo': (0.0, 0.1)}
    factors = {'L0_attn_Wq': 7.041,
     'L0_attn_Wk': 8.0,
     'L0_attn_Wv': 8.0,
     'L0_attn_Wo': 6.774,
     'L0_ffn_W_r': 3.152,
     'L0_ffn_mu_r': 6.389}
    for name, (base, spread) in spreads.items():
        noise = np.random.default_rng([zlib.crc32(name.encode()), seed]).standard_normal(out[name].shape)
        drawn = base * np.exp(spread * noise) if base else spread * noise
        out[name] = jnp.asarray(drawn.astype(out[name].dtype))
    for name, factor in factors.items():
        out[name] = (out[name] * factor).astype(out[name].dtype)
    return out
```

```python
from contextlib import ExitStack

import concourse.bass as bass
from concourse import mybir

F32 = mybir.dt.float32
BF16 = mybir.dt.bfloat16
F16 = mybir.dt.float16
I32 = mybir.dt.int32
ALU = mybir.AluOpType
ACT = mybir.ActivationFunctionType

NB, L, D, H, DH = 2, 4096, 256, 16, 16
NT = L // 128
U = max(1, min(512, int(0.6 * 512)))
SCALE = 0.25
EPS = 1e-5
A_COLS = (U + 15) // 16
CH = [(0, 128), (128, 128), (256, U - 256)]
KORD = [0, 1, 0, 2, 0, 1]
QORD = [0, 0, 1, 0, 2, 1]
GROUPS = [(0, 0, 8), (0, 8, 8), (1, 0, 8), (1, 8, 6), (1, 14, 2)]
NE = 6
PVLAG = 4


class Engine:

    def __init__(self, sem):
        self.sem, self.n, self.q, self.seen = sem, 0, [], {}

    def waits(self, toks):
        for t in toks:
            if t is None:
                continue
            s, v = t
            if self.seen.get(id(s), 0) < v:
                self.seen[id(s)] = v
                self.q.append(("w", s, v))

    def do(self, f, *toks):
        self.waits(toks)
        self.n += 1
        self.q.append(("i", f, self.sem, 1))
        return (self.sem, self.n)

    def quiet(self, f, *toks):
        self.waits(toks)
        self.q.append(("i", f, None, 0))

    def run(self, e):
        for item in self.q:
            if item[0] == "w":
                e.wait_ge(item[1], item[2])
            else:
                r = item[1](e)
                if item[2] is not None:
                    r.then_inc(item[2], item[3])


class Line:

    def __init__(self, sem):
        self.sem, self.n = sem, 0

    def dma(self, eng, f, *toks):
        eng.waits(toks)
        self.n += 16
        eng.q.append(("i", f, self.sem, 16))
        return (self.sem, self.n)

    @property
    def all(self):
        return (self.sem, self.n) if self.n else None


class Ring:

    def __init__(self, slots):
        self.slots, self.free, self.i = slots, [None] * len(slots), 0

    def take(self):
        s = self.i % len(self.slots)
        self.i += 1
        return s, self.slots[s], self.free[s]


def attention_rwkv(nc, x, Wq, bq, Wk, bk, Wv, bv, Wo, bo, W_r, W_k, W_v, mu_r, mu_k, out):
    ctx = ExitStack()
    with ctx:
        def sb(name, shape, dt=F32):
            return ctx.enter_context(nc.sbuf_tensor(name, shape, dt))

        def sem(name):
            return ctx.enter_context(nc.semaphore(name))

        def line(name):
            return Line(sem(name))

        pe, act, dve, pool, sp = (Engine(sem("s_" + n)) for n in ("pe", "act", "dve", "pool", "sp"))

        QSC = nc.dram_tensor("QSC", [NB, 3, D, L], BF16, kind="Internal").ap()
        KSC = nc.dram_tensor("KSC", [NB, 3, 2, D, L // 2], BF16, kind="Internal").ap()
        QN, MT, AO = ([nc.dram_tensor(f"{n}{b}", [L, w], F32, kind="Internal").ap() for b in range(NB)]
                      for n, w in (("QN", D), ("MT", H), ("AO", D)))
        IDX = nc.dram_tensor("IDX", [len(GROUPS), 8, 384], I32, kind="Internal").ap()
        QNr, AOr = ([v.rearrange("n (h d) -> (n h) d", d=DH) for v in vs] for vs in (QN, AO))
        MTr = [v.rearrange("n (h o) -> (n h) o", o=1) for v in MT]

        XT = sb("XT", [128, 2, L + 1])
        VS = sb("VS", [128, NT, H, DH + 1])
        KS = [sb(f"KS{i}", [128, 2, L // 2], BF16) for i in range(2)]
        QS = [sb(f"QS{i}", [128, L], BF16) for i in range(2)]
        KA = sb("KA", [128, 2, L // 2], BF16)
        AB = [sb(f"AB{i}", [128, 1024]) for i in range(3)]
        JK = [sb(f"JK{i}", [128, 1024], BF16) for i in range(2)]
        E = [sb(f"E{i}", [128, U]) for i in range(NE)]
        W2 = {n: sb("W_" + n, [128, 2, D]) for n in ("k", "o", "rT", "kT", "vT")}
        WVQ = sb("WVQ", [128, 2, 2 * D])
        W2["q"] = WVQ[:, :, D:2 * D]
        ident = sb("ident", [128, 128])
        identb = sb("identb", [128, 128], BF16)
        onesb = sb("onesb", [128, 128], BF16)
        trib = sb("trib", [128, 128], BF16)
        cols = sb("cols", [128, 16])
        bvb = sb("bvb", [128, D])
        bqb = sb("bqb", [128, D])
        bob = sb("bob", [128, D])
        zero = sb("zero", [128, D])
        tokc = sb("tokc", [128, NT], F16)
        halfc = sb("halfc", [128, 4])
        xin = [sb(f"xin{i}", [128, 4, D]) for i in range(2)]
        xpart = sb("xpart", [128, 2, 8])
        xbar = sb("xbar", [128, 2])
        SCR = sb("SCR", [128, 5632])
        kf = SCR[:, 0:1024]
        kr = SCR[:, 1024:2048]
        sp3 = [[SCR[:, 2048 + 512 * (3 * i + s):2560 + 512 * (3 * i + s)].bitcast(BF16) for s in range(3)]
               for i in range(2)]
        ksb = SCR[:, 5120:5632]
        SPr = sb("SPr", [128, NT, 8, 2])
        S = sb("S", [128, NT, 8])
        dif = sb("dif", [128, NT, 8])
        msk = sb("msk", [128, NT, 8], BF16)
        msk2 = sb("msk2", [128, NT, 8], BF16)
        msk3 = sb("msk3", [128, NT, 8], BF16)
        cand = sb("cand", [128, 8], I32)
        vbit = sb("vbit", [128, 8], I32)
        need = sb("need", [128, 8])
        slotf = dif
        sloti = sb("sloti", [128, NT, 8], I32)
        sla = sloti
        slb = sb("slb", [128, NT, 8], I32)
        fa = sb("fa", [128, NT * 8], F16)
        fb = sb("fb", [128, NT * 8], F16)
        OA = SCR[:, 2048:2048 + A_COLS * NT * 4].bitcast(F16).rearrange("p (a n) -> p a n", a=A_COLS)
        OB = SCR[:, 0:16 * NT * 4].bitcast(F16).rearrange("p (a n) -> p a n", a=16)
        hoff = sb("hoff", [A_COLS, 8, 16], I32)
        idw = sb("idw", [A_COLS, 8, 16], I32)
        idxs = [sb(f"idxs{i}", [128, 8, 3], I32) for i in range(2)]
        QG = sb("QG", [128, 24, DH])
        MG = sb("MG", [128, 24])
        QH = sb("QH", [128, 24, DH])
        MH = sb("MH", [128, 24])
        QST = sb("QST", [128, 24, 128], BF16)
        QT = [sb(f"QT{i}", [128, 320], BF16) for i in range(2)]
        QTn = [sb(f"QTn{i}", [128, 320], BF16) for i in range(2)]
        OT = [sb(f"OT{i}", [DH + 1, 384]) for i in range(2)]
        rec = sb("rec", [128, 3])
        OG = [sb(f"OG{i}", [128, 3, DH]) for i in range(2)]
        fx = [xin[i][:, 0, :] for i in range(2)]
        fao = [xin[i][:, 1, :] for i in range(2)]
        fo = [xin[i][:, 2, :] for i in range(2)]
        cut = [SCR[:, D * i:D * i + D] for i in range(9)]
        fh, fx1, fr = cut[0:3]
        faT, fm0, fm1, fmp, fk, fk2 = (c.rearrange("p (k n) -> p k n", k=2) for c in cut[3:9])
        fm = [fm0, fm1]
        fst = sb("fst", [128, 6])
        fmv = sb("fmv", [128, 2])
        frs = sb("frs", [128, 2])

        CP = ctx.enter_context(nc.psum_tensor("CP", [128, 3, 512], F32))
        PV = ctx.enter_context(nc.psum_tensor("PV", [128, 512], F32))
        DP = ctx.enter_context(nc.psum_tensor("DP", [128, 2, 1024], F32))
        C = Ring([CP[:, i, :] for i in range(3)])
        DR = Ring([DP[:, i, :] for i in range(2)])

        def fill(ring, mms, *toks):
            s, slot, free = ring.take()
            pe.waits((free,) + toks)
            for n, (o, a, b, st, en) in enumerate(mms):
                f = lambda e, o=o(slot), a=a, b=b, st=st, en=en: e.matmul(o, a, b, start=st, stop=en)
                if n == len(mms) - 1:
                    t = pe.do(f)
                else:
                    pe.quiet(f)
            return s, slot, t

        def turn(ring, trs, *toks):
            s, slot, free = ring.take()
            pe.waits((free,) + toks)
            for n, (o, a, i) in enumerate(trs):
                f = lambda e, o=o(slot), a=a, i=i: e.transpose(o, a, i)
                if n == len(trs) - 1:
                    t = pe.do(f)
                else:
                    pe.quiet(f)
            return s, slot, t

        l_w = line("l_w")
        l_z = line("l_z")
        t_zero = pool.do(lambda e: e.memset(zero[:], 0.0))
        pool.do(lambda e: e.memset(ident[:], 0.0))
        pool.do(lambda e: e.memset(onesb[:], 1.0))
        pool.do(lambda e: e.memset(halfc[:, 0:1], -0.5))
        t = pool.do(lambda e: e.memset(halfc[:, 1:2], EPS))
        pool.do(lambda e: e.affine_select(out=ident[:], in_=ident[:], compare_op=ALU.not_equal, fill=1.0, base=0,
                                          pattern=[[-1, 128]], channel_multiplier=1), t)
        t = pool.do(lambda e: e.affine_select(out=trib[:], in_=onesb[:], compare_op=ALU.is_ge, fill=0.0, base=0,
                                              pattern=[[1, 128]], channel_multiplier=-1))
        t_id = pool.do(lambda e: e.tensor_copy(identb[:], ident[:]), t)
        pool.do(lambda e: e.iota(tokc[:], pattern=[[128, NT]], base=-L // 2, channel_multiplier=1,
                                 allow_small_or_imprecise_dtypes=True))
        pool.do(lambda e: e.memset(QG[:], 0.0))
        pool.do(lambda e: e.memset(MG[:], 0.0))
        pool.do(lambda e: e.memset(QST[:], 0.0))
        for i in range(2):
            pool.do(lambda e, i=i: e.memset(OT[i][:], 1.0))
        t = pool.do(lambda e: e.memset(KA[96:128, 0, :], 1.0), (pool.sem, pool.n))
        pool.waits([t])
        t_const = pool.do(lambda e: e.memset(VS[:, :, :, DH:DH + 1], 1.0))

        def wload(dst, src):
            return l_w.dma(sp, lambda e: e.dma_start(dst, src))

        for n, w in (("k", Wk), ("o", Wo)):
            wload(W2[n][:], w.rearrange("(k p) n -> p k n", p=128))
        wload(WVQ[:, :, 0:D], Wv.rearrange("(k p) n -> p k n", p=128))
        wload(WVQ[:, :, D:2 * D], Wq.rearrange("(k p) n -> p k n", p=128))
        raw = {"rT": (AB[0], W_r), "kT": (AB[1], W_k), "vT": (AB[2], W_v)}
        for n, (buf, w) in raw.items():
            wload(buf[:, 0:512].rearrange("p (k c) -> p k c", k=2), w.rearrange("(k p) c -> p k c", p=128))
        BQ, BK, MR, MK, SH, MR1, MK1, KB = (slice(2 * i, 2 * i + 2) for i in range(8))
        for c, v in ((BQ, bq), (BK, bk), (MR, mu_r), (MK, mu_k)):
            for k in range(2):
                wload(cols[:, c.start + k:c.start + k + 1], v[128 * k:128 * k + 128].unsqueeze(1))
        for d, v in ((bvb, bv), (bqb, bq), (bob, bo)):
            wload(d[:], v.partition_broadcast(128))
        t_w = l_w.all
        t_kw = pool.do(lambda e: e.tensor_scalar(W2["k"][:], W2["k"][:], 0.5, None, ALU.mult), t_w)
        pool.do(lambda e: e.tensor_scalar(cols[:, BK], cols[:, BK], 0.5, None, ALU.mult), t_w)
        pool.do(lambda e: e.tensor_scalar(cols[:, MR1], cols[:, MR], -1.0, 1.0, ALU.mult, ALU.add))
        t_cols = pool.do(lambda e: e.tensor_scalar(cols[:, MK1], cols[:, MK], -1.0, 1.0, ALU.mult, ALU.add))
        t_ffw = None
        for n, (buf, w) in raw.items():
            src = buf[:, 0:512].rearrange("p (k c) -> p k c", k=2)
            trs = [(lambda s, i=i, j=j: s[:, (2 * i + j) * 128:(2 * i + j + 1) * 128],
                    src[:, j, 128 * i:128 * i + 128], ident[:]) for i in range(2) for j in range(2)]
            s, slot, tp = turn(C, trs, t_w, t_id)
            t_ffw = C.free[s] = act.do(lambda e, n=n, slot=slot: e.activation(
                W2[n][:].rearrange("p k c -> p (k c)"), slot, ACT.Copy, scale=0.5 if n == "vT" else 1.0), tp)
        zs = zero[:].unsqueeze(1).broadcast_to([128, NT, D])
        for b in range(NB):
            l_z.dma(sp, lambda e, b=b: e.dma_start(AO[b].rearrange("(t p) c -> p t c", p=128), zs), t_zero)
            l_z.dma(sp, lambda e, b=b: e.dma_start(
                MT[b].rearrange("n h -> (n h)").rearrange("(p a c) -> p a c", p=128, a=2),
                zero[:].unsqueeze(1).broadcast_to([128, 2, D])), t_zero)

        l_x = [line(f"l_x{i}") for i in range(2)]
        l_s = [line(f"l_s{i}") for i in range(2)]
        l_q = [line(f"l_q{i}") for i in range(2)]
        t_xin = [None, None]
        t_kf = [None]
        t_sp = [0]
        ready = {}
        xt_free = [None]

        def split(src_t, fast):
            i = t_sp[0] % 2
            t_sp[0] += 1
            hi, mid, lo = sp3[i]
            old = l_s[i].all
            a, d = (act, dve) if fast else (pool, pool)
            if fast:
                t1 = a.do(lambda e: e.copy(hi[:], kf[:]), src_t, old)
            else:
                t1 = a.do(lambda e: e.tensor_copy(hi[:], kf[:]), src_t, old)
            t2 = d.do(lambda e: e.tensor_tensor(kr[:], kf[:], hi[:], ALU.subtract), t1, src_t)
            if fast:
                t3 = a.do(lambda e: e.copy(mid[:], kr[:]), t2)
            else:
                t3 = a.do(lambda e: e.tensor_copy(mid[:], kr[:]), t2)
            t4 = d.do(lambda e: e.tensor_tensor(lo[:], kr[:], mid[:], ALU.subtract), t3, old)
            t_kf[0] = t4
            return i, (t1, t3, t4)

        def project(b):
            xb = x[b]
            fast = b == 0
            for c in range(8):
                i = c % 2
                t = l_x[i].dma(sp, lambda e, c=c, i=i: e.dma_start(
                    xin[i][:], xb[c * 512:(c + 1) * 512, :].rearrange("(j p) c -> p j c", p=128)), t_xin[i])
                for k in range(2):
                    trs = [(lambda s, j=j: s[:, 128 * j:128 * j + 128], xin[i][:, j, 128 * k:128 * k + 128], ident[:])
                           for j in range(4)]
                    s, slot, tp = turn(C, trs, t, t_id)
                    t_xin[i] = tp
                    t_xt = C.free[s] = act.do(lambda e, c=c, k=k, slot=slot: e.activation(
                        XT[:, k, 1 + c * 512:1 + (c + 1) * 512], slot, ACT.Copy, accum_out=xpart[:, k, c:c + 1]),
                        tp, xt_free[0])
                    yield
            t = dve.do(lambda e: e.reduce_sum(xbar[:], xpart[:], mybir.AxisListType.X), t_xt)
            t = dve.do(lambda e: e.tensor_scalar(xbar[:], xbar[:], 1.0 / L, None, ALU.mult), t)
            mms = [(lambda s, h=h: s[:, h:h + 1], W2["k"][:, k, 128 * h:128 * h + 128], xbar[:, k:k + 1], k == 0, k == 1)
                   for h in range(2) for k in range(2)]
            yield
            s, slot, tp = fill(DR, mms, t, t_kw)
            t = dve.do(lambda e, slot=slot: e.tensor_tensor(cols[:, KB], slot[:, 0:2], cols[:, BK], ALU.add), tp, t_cols)
            DR.free[s] = t
            t_sh = dve.do(lambda e: e.tensor_tensor(cols[:, SH], cols[:, BK], cols[:, KB], ALU.subtract), t)
            yield
            for half in range(2):
                hs = slice(128 * half, 128 * half + 128)

                def mms_of(w, c):
                    return [(lambda s: s[:, 0:512], w[:, k, hs], XT[:, k, 1 + c * 512:1 + (c + 1) * 512], k == 0, k == 1)
                            for k in range(2)]
                sh = cols[:, SH.start + half:SH.start + half + 1]
                bqc = cols[:, BQ.start + half:BQ.start + half + 1]
                for c in range(4):
                    s, slot, tp = fill(C, mms_of(W2["k"], c + 4), t_xt, t_kw)
                    t1 = C.free[s] = act.do(lambda e, slot=slot, sh=sh: e.activation(
                        ksb[:], slot, ACT.Identity, bias=sh), tp, t_sh, t_kf[0])
                    yield
                    s, slot, tp = fill(DR, mms_of(W2["k"], c))
                    dve.do(lambda e, slot=slot, sh=sh: e.scalar_tensor_tensor(
                        out=kf[:, 0:512], in0=slot[:, 0:512], scalar=sh, in1=ksb[:], op0=ALU.add, op1=ALU.add),
                        tp, t1, t_kf[0])
                    t = DR.free[s] = dve.do(lambda e, slot=slot, sh=sh: e.scalar_tensor_tensor(
                        out=kf[:, 512:1024], in0=slot[:, 0:512], scalar=sh, in1=ksb[:], op0=ALU.add, op1=ALU.subtract))
                    yield
                    i, ts = split(t, fast)
                    for m in range(3):
                        l_s[i].dma(sp, lambda e, m=m, i=i, c=c, hs=hs: e.dma_start(
                            KSC[b, m, :, hs, c * 512:(c + 1) * 512].rearrange("m p n -> p m n"),
                            sp3[i][m][:].rearrange("p (m n) -> p m n", m=2)), ts[m])
                    yield
                    yield
                    yield
                for c in range(4):
                    for j in range(2):
                        s, slot, tp = fill(C, mms_of(W2["q"], 2 * c + j), t_w)
                        t = C.free[s] = act.do(lambda e, slot=slot, bqc=bqc, j=j: e.activation(
                            kf[:, 512 * j:512 * j + 512], slot, ACT.Identity, bias=bqc), tp, t_kf[0])
                        yield
                    i, ts = split(t, fast)
                    for m in range(3):
                        l_s[i].dma(sp, lambda e, m=m, i=i, c=c, hs=hs: e.dma_start(
                            QSC[b, m, hs, c * 1024:(c + 1) * 1024], sp3[i][m][:]), ts[m])
                    yield
                    yield
                    yield
                ready[b, half] = (l_s[0].all, l_s[1].all)

        vs_free = [None]
        t_vs = {}

        def values(b):
            for t in range(NT):
                i = (t // 4) % 2
                mms = [(lambda s: s, XT[:, k, 1 + 128 * t:129 + 128 * t], WVQ[:, k, :], k == 0, k == 1)
                       for k in range(2)]
                s, slot, tp = fill(C, mms, t_w)
                act.do(lambda e, slot=slot, t=t: e.copy(
                    VS[:, t, :, 0:DH], slot[:, 0:D].rearrange("p (h d) -> p h d", d=DH)), tp, vs_free[0], t_const)
                ta = C.free[s] = act.do(lambda e, slot=slot, t=t, i=i: e.copy(xin[i][:, t % 4, :], slot[:, D:2 * D]),
                                        l_q[i].all, t_xin[i])
                if t % 4 == 3:
                    l_q[i].dma(sp, lambda e, t=t, i=i: e.dma_start(
                        QN[b][(t - 3) * 128:(t + 1) * 128, :].rearrange("(j p) c -> p j c", p=128),
                        xin[i][:]), ta)
                yield
                yield
            t_xin[0], t_xin[1] = l_q[0].all, l_q[1].all
            t_vs[b] = ta
            xt_free[0] = tp
            ready["v", b] = (l_q[0].all, l_q[1].all)

        l_k = [line(f"l_k{i}") for i in range(2)]
        t_head = [None, None]
        t_ab = [None] * 3
        t_jk = [None] * 2
        kper = [0]

        def load_stack(ln, ks, b, h, *toks):
            hr = slice(16 * h, 16 * h + 16)
            for r, m in enumerate(KORD):
                ln.dma(sp, lambda e, r=r, m=m: e.dma_start(
                    ks[16 * r:16 * r + 16, :, :], KSC[b, m, :, hr, :].rearrange("m p n -> p m n")), *toks)

        def load_head(n):
            b, h = divmod(n, H)
            i = n % 2
            w = (t_head[i],) + ready[b, h // 8]
            load_stack(l_k[i], KS[i], b, h, *w)
            for r, m in enumerate(QORD):
                l_k[i].dma(sp, lambda e, r=r, m=m, h=h: e.dma_start(
                    QS[i][16 * r:16 * r + 16, :], QSC[b, m, 16 * h:16 * h + 16, :]), *w)

        t_sp_free = [None]

        def here():
            return tuple((e.sem, e.n) for e in (pe, act, dve, pool) if e.n)

        def period(n, g, hl, t, u):
            i = n % 2
            k = kper[0]
            kper[0] += 1
            q = QS[i][0:96, 128 * t:128 * t + 128]
            ld = l_k[i].all
            ab, jk = AB[k % 3], JK[k % 2]
            for j in range(2):
                c0 = 1024 * u + 512 * j
                s, slot, tp = fill(C, [(lambda s: s, q, KS[i][0:96, 1, c0:c0 + 512], True, True)], ld)
                ta = C.free[s] = act.do(lambda e, slot=slot, j=j, ab=ab: e.activation(
                    ab[:, 512 * j:512 * j + 512], slot, ACT.Abs), tp, t_ab[k % 3], t_ffw)
            mms = [(lambda s, j=j: s[:, 512 * j:512 * j + 512], q,
                    KS[i][0:96, 0, 1024 * u + 512 * j:1024 * u + 512 * j + 512], True, True) for j in range(2)]
            s, slot, tp = fill(DR, mms)
            t_head[i] = tp
            w = t_sp_free[0] if (t, u, hl) == (0, 0, 0) else None
            td = dve.do(lambda e, slot=slot: e.tensor_tensor_reduce(
                out=jk[:], in0=slot, in1=ab[:], scale=1.0, scalar=-3.0e38, op0=ALU.add, op1=ALU.max,
                accum_out=SPr[:, t, hl, u:u + 1]), tp, ta, t_jk[k % 2], w)
            DR.free[s] = t_ab[k % 3] = t_jk[k % 2] = td
            return td

        l_m = line("l_m")
        l_i = line("l_i")
        l_g = line("l_g")
        l_a = line("l_a")
        l_o = [line(f"l_o{i}") for i in range(2)]
        st = {"ka": None, "qt": [None, None], "pv": None, "e": [None] * NE, "ne": 0, "na": 0,
              "s": None, "ot": [None, None], "qst": None, "og": None, "idx": [(), ()], "ix": None}

        def prefix(m, n, tm):
            mms = [(lambda s: s[:, 0:NT * n], trib[:], m, True, False)]
            for t in range(NT - 1):
                r = m[:, t:t + 1, :].broadcast_to([128, NT - 1 - t, n])
                mms.append((lambda s, t=t: s[:, (t + 1) * n:NT * n], onesb[:], r, False, t == NT - 2))
            return fill(DR, mms, tm, t_id)

        def select(g, t_spars, slow):
            b, h0, n = GROUPS[g]
            edge = here()
            sg, dg = S[:, :, 0:n], dif[:, :, 0:n]
            m1, m2, m3 = (m[:].rearrange("p t h -> p (t h)")[:, 0:NT * n].rearrange("p (t h) -> p t h", h=n)
                          for m in (msk, msk2, msk3))
            cd = cand[:, 0:n]
            cf = cand[:].bitcast(F32)[:, 0:n].unsqueeze(1).broadcast_to([128, NT, n])
            sp_ = SPr
            t = dve.do(lambda e: e.scalar_tensor_tensor(
                out=sg, in0=sp_[:, :, 0:n, 0], scalar=0.0, in1=sp_[:, :, 0:n, 1], op0=ALU.max, op1=ALU.max),
                t_spars, st["s"], l_m.all)
            t_s = t
            t_sp_free[0] = t
            MTb = MT[b][:, h0:h0 + n].rearrange("(t p) h -> p t h", p=128)
            t_m = l_m.dma(sp, lambda e: e.dma_start(MTb, sg), t, l_z.all)
            t = dve.do(lambda e: e.memset(cd, 1 << 30))
            tp_free = None
            for bit in range(30, -1, -1):
                t1 = pool.do(lambda e: e.tensor_tensor(dg, sg, cf, ALU.subtract), t, t_s)
                t1 = pool.do(lambda e: e.tensor_scalar(m1, dg, 0.0, None, ALU.is_ge), t1, tp_free)
                for _ in range(3 * slow):
                    yield
                s, slot, tp = fill(DR, [(lambda s: s[:, 0:n], onesb[:], m1[:, j, :], j == 0, j == NT - 1)
                                        for j in range(NT)], t1)
                tp_free = tp
                t2 = DR.free[s] = dve.do(lambda e, slot=slot, bit=bit: e.tensor_scalar(
                    vbit[:, 0:n], slot[:, 0:n], float(U), float(1 << bit), ALU.is_lt, ALU.mult), tp)
                t = dve.do(lambda e, bit=bit: e.scalar_tensor_tensor(
                    out=cd, in0=vbit[:, 0:n], scalar=(1 << bit) >> 1, in1=cd,
                    op0=ALU.bitwise_xor, op1=ALU.bitwise_xor), t2)
                if slow:
                    yield
            t = pool.do(lambda e: e.tensor_tensor(dg, sg, cf, ALU.subtract), t)
            t1 = pool.do(lambda e: e.tensor_scalar(m1, dg, 0.0, None, ALU.is_gt), t, tp_free)
            t2 = pool.do(lambda e: e.tensor_scalar(m2, dg, 0.0, None, ALU.is_equal), t)
            for _ in range(3 * slow):
                yield
            s, slot, tp = fill(DR, [(lambda s: s[:, 0:n], onesb[:], m1[:, j, :], j == 0, j == NT - 1)
                                    for j in range(NT)], t1)
            t = DR.free[s] = dve.do(lambda e, slot=slot: e.tensor_scalar(need[:, 0:n], slot[:, 0:n], -1.0, float(U),
                                                              ALU.mult, ALU.add), tp)
            s, slot, tp = prefix(m2, n, t2)
            nb = need[:, 0:n].unsqueeze(1).broadcast_to([128, NT, n])
            t = DR.free[s] = dve.do(lambda e, slot=slot: e.tensor_tensor(
                m3, slot[:, 0:NT * n].rearrange("p (t h) -> p t h", h=n), nb, ALU.is_le), tp, t)
            t = dve.do(lambda e: e.tensor_tensor(m3, m3, m2, ALU.mult), t)
            t = dve.do(lambda e: e.tensor_tensor(m3, m3, m1, ALU.add), t)
            for _ in range(2 * slow):
                yield
            s, slot, tp = prefix(m3, n, t)
            sf, si = (q[:].rearrange("p t h -> p (t h)")[:, 0:NT * n] for q in (slotf, sloti))
            ai, bi = (q[:].rearrange("p t h -> p (t h)")[:, 0:NT * n] for q in (sla, slb))
            m3f = msk3[:].rearrange("p t h -> p (t h)")[:, 0:NT * n]
            t = DR.free[s] = dve.do(lambda e, slot=slot: e.tensor_tensor(sf, slot[:, 0:NT * n], m3f, ALU.mult), tp)
            if slow:
                yield
            t = dve.do(lambda e: e.tensor_scalar(si, sf, -1.0, None, ALU.add), t)
            t2 = dve.do(lambda e: e.tensor_scalar(bi, si, 15, None, ALU.bitwise_and), t)
            t1 = dve.do(lambda e: e.tensor_scalar(ai, si, 4, None, ALU.arith_shift_right), t2)
            t1 = pool.do(lambda e: e.tensor_copy(fa[:, 0:NT * n], ai), t1)
            t2 = pool.do(lambda e: e.tensor_copy(fb[:, 0:NT * n], bi), t2)
            tk = tokc[:].unsqueeze(2).broadcast_to([128, NT, n])
            for _ in range(2 * slow):
                yield
            t_m2 = []
            for j in range(16):
                t = dve.do(lambda e, j=j: e.tensor_scalar(OB[:, j, 0:NT * n], fb[:, 0:NT * n], float(j), None,
                                                          ALU.is_equal), t2, *edge)
                v = OB[:, j, 0:NT * n].rearrange("p (t h) -> p t h", h=n)
                t_b = pool.do(lambda e, v=v: e.tensor_tensor(v, v, tk, ALU.mult), t)
                if slow and j % 4 == 3:
                    yield
            for j in range(A_COLS):
                t_a = dve.do(lambda e, j=j: e.tensor_scalar(OA[:, j, 0:NT * n], fa[:, 0:NT * n], float(j), None,
                                                            ALU.is_equal), t1)
                if slow and j % 4 == 3:
                    yield
            for _ in range(3 * slow):
                yield
            t_ho = pool.do(lambda e: e.iota(hoff[:], pattern=[[1, 8], [0, 16]], base=16 * (L // 2) + h0,
                                            channel_multiplier=0), *edge)
            for h in range(n):
                mms = [(lambda s: s[0:A_COLS, 0:16], OA[:, :, n * j + h], OB[:, :, n * j + h], j == 0, j == NT - 1)
                       for j in range(NT)]
                s, slot, tp = fill(DR, mms, t_a, t_b)
                t = DR.free[s] = dve.do(lambda e, slot=slot, h=h: e.scalar_tensor_tensor(
                    out=idw[:, h, :], in0=slot[0:A_COLS, 0:16], scalar=16.0, in1=hoff[:, h, :],
                    op0=ALU.mult, op1=ALU.add), tp, l_i.all, t_ho)
                if slow:
                    yield
            st["ix"] = tp
            t = l_i.dma(sp, lambda e: e.dma_start(
                IDX[g, 0:n, 0:16 * A_COLS].rearrange("h (a b) -> a h b", b=16), idw[:, 0:n, :]), t)
            ix = idxs[g % 2]
            tw = t
            for c, (a0, w) in enumerate(CH):
                t = l_i.dma(sp, lambda e, c=c, a0=a0, w=w: e.dma_start(
                    ix[0:w, 0:n, c], IDX[g, 0:n, a0:a0 + w].rearrange("h s -> s h")), tw, *st["idx"][g % 2])
            for _ in range(6 * slow):
                yield
            ixf = ix[:].rearrange("p h c -> p (h c)")
            for h in range(n):
                for c, (_, w) in enumerate(CH):
                    k = 3 * h + c
                    l_g.dma(pool, lambda e, k=k, w=w: e.indirect_dma_start(
                        out=QG[0:w, k, :], out_offset=None, in_=QNr[b],
                        in_offset=bass.IndirectOffsetOnAxis(ap=ixf[0:w, k:k + 1], axis=0)),
                        t, t_m, st["qst"], *ready["v", b])
                    l_g.dma(pool, lambda e, k=k, w=w: e.indirect_dma_start(
                        out=MG[0:w, k:k + 1], out_offset=None, in_=MTr[b],
                        in_offset=bass.IndirectOffsetOnAxis(ap=ixf[0:w, k:k + 1], axis=0)))
                    if slow:
                        yield
            for _ in range(3 * slow):
                yield
            hc = 3 * n
            q, r = QG[:, 0:hc, :], QH[:, 0:hc, :]
            z = [QST[:, 0:hc, 16 * k:16 * k + 16] for k in range(6)]
            bq4 = bqb[:, DH * h0:DH * (h0 + n)].rearrange("p (h d) -> p h d", d=DH)
            for c in range(3):
                qc = QG[:].rearrange("p (h c) d -> p h c d", c=3)[:, 0:n, c, :]
                t = pool.do(lambda e, qc=qc: e.tensor_tensor(qc, qc, bq4, ALU.add), l_g.all, t_w)
            t = pool.do(lambda e: e.tensor_copy(z[0], q), t, st["qst"])
            pool.do(lambda e: e.tensor_copy(z[1], z[0]), t)
            pool.do(lambda e: e.tensor_copy(z[3], z[0]))
            t = pool.do(lambda e: e.tensor_tensor(r, q, z[0], ALU.subtract))
            t = pool.do(lambda e: e.tensor_copy(z[2], r), t)
            pool.do(lambda e: e.tensor_copy(z[5], z[2]), t)
            pool.do(lambda e: e.tensor_tensor(z[4], r, z[2], ALU.subtract))
            mz = [QST[:, 0:hc, 96 + k] for k in range(3)]
            m, mr = MG[:, 0:hc], MH[:, 0:hc]
            t = pool.do(lambda e: e.tensor_scalar(mr, m, -1.0, None, ALU.mult))
            t = pool.do(lambda e: e.tensor_copy(mz[0], mr), t)
            t = pool.do(lambda e: e.tensor_tensor(mr, mr, mz[0], ALU.subtract), t)
            t = pool.do(lambda e: e.tensor_copy(mz[1], mr), t)
            t_q = pool.do(lambda e: e.tensor_tensor(mz[2], mr, mz[1], ALU.subtract), t)
            st["s"] = t_q
            for _ in range(4 * slow):
                yield

            pend = []

            def flush(lim, h):
                while len(pend) > lim:
                    j, tile, te = pend.pop(0)
                    first, last = tile == 0, tile == 2 * 16 - 1
                    tp = pe.do(lambda e, j=j, tile=tile, first=first, last=last: e.matmul(
                        PV[0:DH + 1, 0:U], VS[:, tile, h, :], E[j][:], start=first, stop=last),
                        te, st["pv"] if first else None, t_vs[b])
                    st["e"][j] = tp
                    st["pvt"] = tp

            def load_ka(h):
                load_stack(l_a, KA, b, h0 + h, st["ka"], t_const,
                           *ready[b, (h0 + h) // 8])

            for hl in range(n):
                h = h0 + hl
                i = h % 2
                load_ka(hl)
                trs = [(lambda s, a=a, w=w: s.bitcast(BF16)[:, a:a + w], QST[0:w, 3 * hl + c, :],
                        identb[0:w, 0:w]) for c, (a, w) in enumerate(CH[:2])]
                trs.append((lambda s: s.bitcast(BF16)[:, 256:256 + CH[2][1] + 1], QST[0:52, 3 * hl + 2, :],
                            identb[0:52, 0:52]))
                s, slot, tp = turn(C, trs, t_q, t_id)
                st["qst"] = tp
                t1 = act.do(lambda e, slot=slot, i=i: e.copy(QT[i][:, 0:U], slot.bitcast(BF16)[:, 0:U]),
                            tp, st["qt"][i])
                t2 = C.free[s] = act.do(lambda e, slot=slot, i=i: e.mul(QTn[i][:, 0:U], slot.bitcast(BF16)[:, 0:U],
                                                                        -1.0))
                ld = l_a.all
                for _ in range(4 * slow):
                    yield
                tiles = []
                for kc in range(16):
                    ks = slice(128 * kc, 128 * kc + 128)
                    for sg_ in range(2):
                        qm = (QT if sg_ == 0 else QTn)[i][0:96, 0:U]
                        mms = [(lambda s: s[:, 0:U], KA[0:99, 0, ks], QT[i][0:99, 0:U], True, False),
                               (lambda s: s[:, 0:U], KA[0:96, 1, ks], qm, False, True)]
                        s, slot, tp = fill(C, mms, t2, ld)
                        j = st["ne"] % NE
                        st["ne"] += 1
                        te = C.free[s] = act.do(lambda e, slot=slot, j=j: e.activation(
                            E[j][:], slot[:, 0:U], ACT.Exp, scale=SCALE), tp, st["e"][j])
                        pend.append((j, kc + 16 * sg_, te))
                        flush(PVLAG, h)
                        if slow:
                            yield
                st["ka"] = st["qt"][i] = tp
                flush(0, h)
                if slow:
                    yield
                t = st["pv"] = act.do(lambda e, i=i: e.copy(OT[i][:, 0:U], PV[0:DH + 1, 0:U]), st["pvt"],
                                      st["ot"][i], t_const)
                for _ in range(2 * slow):
                    yield
                trs = [(lambda s, c=c: s[:, 32 * c:32 * c + DH + 1], OT[i][:, 128 * c:128 * c + 128],
                        ident[0:DH + 1, 0:DH + 1]) for c in range(3)]
                s, slot, tp = turn(DR, trs, t)
                st["ot"][i] = tp
                sv = slot[:, 0:96].rearrange("p (c d) -> p c d", c=3)
                t = dve.do(lambda e, sv=sv: e.reciprocal(rec[:], sv[:, :, DH]), tp, st.get("rec"))
                t = DR.free[s] = dve.do(lambda e, sv=sv, i=i: e.tensor_tensor(
                    OG[i][:], sv[:, :, 0:DH], rec[:].unsqueeze(2).broadcast_to([128, 3, DH]), ALU.mult),
                    t, l_o[i].all)
                st["rec"] = t
                bv3 = bvb[:, DH * h:DH * h + DH].unsqueeze(1).broadcast_to([128, 3, DH])
                t = pool.do(lambda e, i=i, bv3=bv3: e.tensor_tensor(OG[i][:], OG[i][:], bv3, ALU.add), t, t_w)
                for c, (_, w) in enumerate(CH):
                    l_o[i].dma(pool, lambda e, i=i, c=c, w=w, k=3 * hl + c: e.indirect_dma_start(
                        out=AOr[b], out_offset=bass.IndirectOffsetOnAxis(ap=ixf[0:w, k:k + 1], axis=0),
                        in_=OG[i][0:w, c, :], in_offset=None), t, l_z.all)
                if slow:
                    yield
            st["scat"] = st["idx"][g % 2] = (l_o[0].all, l_o[1].all)
            vs_free[0] = st["pvt"]

        l_f = [line(f"l_f{i}") for i in range(2)]
        l_out = [line(f"l_out{i}") for i in range(2)]
        ff = {"x": [None, None], "x1": None, "xm": None, "fh": None, "fr": None, "fk": None, "xt": None}

        def norm(src, t_src, dst, t_dst, slow):
            t = dve.do(lambda e: e.bn_stats(fst[:], src), t_src)
            t = dve.do(lambda e: e.bn_aggr(fmv[:], fst[:]), t, ff.get("mv"))
            for _ in range(2 * slow):
                yield t
            t = pool.do(lambda e: e.tensor_scalar(frs[:, 0:1], fmv[:, 1:2], EPS, None, ALU.add), t)
            t = pool.do(lambda e: e.tensor_tensor(frs[:, 0:1], frs[:, 0:1], halfc[:, 0:1], ALU.pow), t)
            t = pool.do(lambda e: e.tensor_scalar(dst, src, fmv[:, 0:1], frs[:, 0:1], ALU.subtract, ALU.mult),
                        t, t_dst, t_src)
            ff["mv"] = t
            yield t

        def feed(b, scat, slow):
            xb = x[b]
            edge = here()
            tz = pool.do(lambda e: e.memset(XT[:, :, 0:1], 0.0), *edge)
            for e in (act, dve, pool, sp):
                e.waits(edge)

            def load(t):
                i = t % 2
                l_f[i].dma(sp, lambda e: e.dma_start(fx[i][:], xb[128 * t:128 * t + 128, :]), *scat, *t_xin, ff["x"][i], l_out[i].all)
                l_f[i].dma(sp, lambda e: e.dma_start(fao[i][:], AO[b][128 * t:128 * t + 128, :]))
            load(0)
            for t in range(NT):
                i = t % 2
                if t + 1 < NT:
                    load(t + 1)
                ld = l_f[i].all
                s, slot, tp = turn(C, [(lambda s, k=k: s[:, 128 * k:128 * k + 128],
                                        fao[i][:, 128 * k:128 * k + 128], ident[:]) for k in range(2)], ld)
                ta = C.free[s] = act.do(lambda e, slot=slot: e.copy(faT[:].rearrange("p k n -> p (k n)"),
                                                                    slot[:, 0:256]), tp, ff.get("faT"))
                tb = pool.do(lambda e, i=i: e.tensor_tensor(fx[i][:], fx[i][:], bob[:], ALU.add), ld, t_w)
                for _ in range(2 * slow):
                    yield
                s, slot, tp = fill(DR, [(lambda s: s[:, 0:D], faT[:, k, :], W2["o"][:, k, :], k == 0, k == 1)
                                        for k in range(2)], ta, t_w)
                ff["faT"] = tp
                th = DR.free[s] = dve.do(lambda e, slot=slot, i=i: e.tensor_tensor(
                    fh[:], slot[:, 0:D], fx[i][:], ALU.add), tp, tb, ff.get("fh"))
                ff["x"][i] = th
                for tn in norm(fh[:], th, fx1[:], ff.get("x1"), slow):
                    if slow:
                        yield
                ff["fh"] = tn
                t_x1 = tn
                for _ in range(2 * slow):
                    yield
                s, slot, tp = turn(C, [(lambda s, k=k: s[:, 128 * k:128 * k + 128],
                                        fx1[:, 128 * k:128 * k + 128], ident[:]) for k in range(2)], t_x1)
                tc = C.free[s] = act.do(lambda e, slot=slot, t=t: e.copy(
                    XT[:, :, 1 + 128 * t:129 + 128 * t], slot[:, 0:256].rearrange("p (k n) -> p k n", k=2)),
                    tp, xt_free[0])
                cur = [XT[:, k, 1 + 128 * t:129 + 128 * t] for k in range(2)]
                prv = [XT[:, k, 128 * t:128 * t + 128] for k in range(2)]
                tm = []
                for m, (ca, cb) in enumerate(((MR, MR1), (MK, MK1))):
                    for k in range(2):
                        pool.do(lambda e, m=m, k=k, ca=ca, v=cur[k]: e.tensor_scalar(
                            fm[m][:, k, :], v, cols[:, ca.start + k:ca.start + k + 1], None, ALU.mult),
                            tc, tz, ff.get(f"fm{m}"), t_cols)
                        tq = pool.do(lambda e, k=k, cb=cb, v=prv[k]: e.tensor_scalar(
                            fmp[:, k, :], v, cols[:, cb.start + k:cb.start + k + 1], None, ALU.mult),
                            ff.get("fmp"))
                    tq = pool.do(lambda e, m=m: e.tensor_tensor(fm[m][:], fm[m][:], fmp[:], ALU.add), tq)
                    ff["fmp"] = tq
                    tm.append(tq)
                    if slow:
                        yield
                for _ in range(3 * slow):
                    yield
                s, slot, tp = fill(C, [(lambda s: s[:, 0:D], fm[0][:, k, :], W2["rT"][:, k, :], k == 0, k == 1)
                                       for k in range(2)], tm[0], t_ffw)
                ff["fm0"] = tp
                tr = C.free[s] = act.do(lambda e, slot=slot: e.activation(fr[:], slot[:, 0:D], ACT.Tanh, scale=0.5),
                                        tp, ff.get("fr"))
                if slow:
                    yield
                s, slot, tp = fill(C, [(lambda s, m=m: s[:, 128 * m:128 * m + 128],
                                        W2["kT"][:, k, 128 * m:128 * m + 128], fm[1][:, k, :], k == 0, k == 1)
                                       for m in range(2) for k in range(2)], tm[1])
                ff["fm1"] = tp
                tk = C.free[s] = act.do(lambda e, slot=slot: e.activation(
                    fk[:].rearrange("p k n -> p (k n)"), slot[:, 0:256], ACT.Relu), tp, ff.get("fk"))
                tk = pool.do(lambda e: e.tensor_tensor(fk2[:], fk[:], fk[:], ALU.mult), tk, ff.get("fk2"))
                ff["fk"] = tk
                for _ in range(3 * slow):
                    yield
                s, slot, tp = fill(DR, [(lambda s: s[:, 0:D], fk2[:, k, :], W2["vT"][:, k, :], k == 0, k == 1)
                                        for k in range(2)], tk)
                ff["fk2"] = tp
                t1 = DR.free[s] = dve.do(lambda e, slot=slot: e.scalar_tensor_tensor(
                    out=fh[:], in0=fr[:], scalar=1.0, in1=slot[:, 0:D], op0=ALU.add, op1=ALU.mult),
                    tp, tr, ff["fh"])
                ff["fr"] = t1
                for _ in range(1 * slow):
                    yield
                t1 = pool.do(lambda e: e.tensor_tensor(fh[:], fh[:], fx1[:], ALU.add), t1)
                ff["x1"] = t1
                for _ in range(1 * slow):
                    yield
                for tn in norm(fh[:], t1, fo[i][:], l_out[i].all, slow):
                    if slow:
                        yield
                ff["fh"] = tn
                l_out[i].dma(sp, lambda e, i=i, t=t: e.dma_start(out[b, 128 * t:128 * t + 128, :], fo[i][:]), tn)
                yield
            xt_free[0] = pe_last()

        def pe_last():
            return (pe.sem, pe.n)

        def drain(job):
            for _ in job:
                pass

        first = project(0)
        for _ in first:
            if (0, 0) in ready:
                break
        load_head(0)
        drain(first)
        drain(values(0))

        def background():
            yield from project(1)
            yield "ready"

        jobs = []
        queue = []

        def step():
            while queue:
                try:
                    next(queue[0])
                    return
                except StopIteration:
                    queue.pop(0)

        aux = []

        def step_aux():
            while aux:
                try:
                    next(aux[0])
                    return
                except StopIteration:
                    aux.pop(0)

        aux.append(project(1))
        scats = {}

        def select_and_mark(g, tok, slow):
            yield from select(g, tok, slow)
            scats[g] = st["scat"]

        n = 0
        for g, (b, h0, cnt) in enumerate(GROUPS):
            for hl in range(cnt):
                if n == H:
                    while aux:
                        step_aux()
                    load_head(n)
                if n + 1 < NB * H and n + 1 != H:
                    load_head(n + 1)
                for t in range(NT):
                    for u in range(2):
                        td = period(n, g, hl, t, u)
                        step()
                        if u == 0:
                            step_aux()
                n += 1
            while queue:
                step()
            if g == 1:
                pass
            while aux:
                step_aux()
            queue.append(select_and_mark(g, td, 1 if g + 1 < len(GROUPS) else 0))
            step()
            if g == 1:
                def rest():
                    yield from values(1)
                    yield from feed(0, scats[1], 1)
                queue.append(rest())
        while queue or aux:
            step()
            step_aux()
        drain(feed(1, st["scat"], 0))
        for ln in (l_w, l_z, l_m, l_i, l_g, *l_s, *l_q, l_a, *l_o, *l_f, *l_out):
            sp.waits([ln.all])

        ctx.enter_context(nc.allow_non_contiguous_dma(reason="columns, indices and maxima are small"))
        block = ctx.enter_context(nc.Block())
        block.tensor(pe.run)
        block.scalar(act.run)
        block.vector(dve.run)
        block.gpsimd(pool.run)
        block.sync(sp.run)


_INS = ['L0_attn_x', 'L0_attn_Wq', 'L0_attn_bq', 'L0_attn_Wk', 'L0_attn_bk', 'L0_attn_Wv', 'L0_attn_bv',
        'L0_attn_Wo', 'L0_attn_bo', 'L0_ffn_W_r', 'L0_ffn_W_k', 'L0_ffn_W_v', 'L0_ffn_mu_r', 'L0_ffn_mu_k']


def kernel(**inputs):
    import numpy as np
    import concourse.bacc as bacc
    from concourse.bass_utils import run_bass_kernel_spmd as run

    nc = bacc.Bacc("TRN2", target_bir_lowering=False, num_devices=1)
    arrays, args = {}, []
    for name in _INS:
        a = np.ascontiguousarray(inputs[name])
        arrays[f"in_{name}"] = a
        args.append(nc.dram_tensor(f"in_{name}", a.shape, F32, kind="ExternalInput").ap())
    out = nc.dram_tensor("out_0", (NB, L, D), F32, kind="ExternalOutput").ap()
    attention_rwkv(nc, *args, out)
    r = run(nc, [arrays], core_ids=[0])
    return r.results[0]["out_0"]
```

```python
from contextlib import ExitStack

import concourse.bass as bass
from concourse import mybir

F32 = mybir.dt.float32
BF16 = mybir.dt.bfloat16
F16 = mybir.dt.float16
I32 = mybir.dt.int32
ALU = mybir.AluOpType
ACT = mybir.ActivationFunctionType

NB, L, D, H, DH = 2, 4096, 256, 16, 16
NT = L // 128
U = max(1, min(512, int(0.6 * 512)))
SCALE = 0.25
EPS = 1e-5
A_COLS = (U + 15) // 16
CH = [(0, 128), (128, 128), (256, U - 256)]
KORD = [0, 1, 0, 2, 0, 1]
QORD = [0, 0, 1, 0, 2, 1]
GROUPS = [(0, 0, 8), (0, 8, 8), (1, 0, 8), (1, 8, 4), (1, 12, 4)]
BUDGET = 0.55
WS = 64.0
NE = 10
PVLAG = 6


class Engine:

    def __init__(self, sem):
        self.sem, self.n, self.q, self.seen = sem, 0, [], {}

    def waits(self, toks):
        for t in toks:
            if t is None:
                continue
            s, v = t
            if self.seen.get(id(s), 0) < v:
                self.seen[id(s)] = v
                self.q.append(("w", s, v))

    def do(self, f, *toks):
        self.waits(toks)
        self.n += 1
        self.q.append(("i", f, self.sem, 1))
        return (self.sem, self.n)

    def quiet(self, f, *toks):
        self.waits(toks)
        self.q.append(("i", f, None, 0))

    def run(self, e):
        for item in self.q:
            if item[0] == "w":
                e.wait_ge(item[1], item[2])
            else:
                r = item[1](e)
                if item[2] is not None:
                    r.then_inc(item[2], item[3])


class Line:

    def __init__(self, sem):
        self.sem, self.n = sem, 0

    def dma(self, eng, f, *toks):
        eng.waits(toks)
        self.n += 16
        eng.q.append(("i", f, self.sem, 16))
        return (self.sem, self.n)

    @property
    def all(self):
        return (self.sem, self.n) if self.n else None


class Ring:

    def __init__(self, slots):
        self.slots, self.free, self.i = slots, [()] * len(slots), 0

    def take(self):
        s = self.i % len(self.slots)
        self.i += 1
        return s, self.slots[s], self.free[s]


def attention_rwkv(nc, x, Wq, bq, Wk, bk, Wv, bv, Wo, bo, W_r, W_k, W_v, mu_r, mu_k, out):
    ctx = ExitStack()
    with ctx:
        def sb(name, shape, dt=F32):
            return ctx.enter_context(nc.sbuf_tensor(name, shape, dt))

        def sem(name):
            return ctx.enter_context(nc.semaphore(name))

        def line(name):
            return Line(sem(name))

        pe, act, dve, pool, sp = (Engine(sem("s_" + n)) for n in ("pe", "act", "dve", "pool", "sp"))

        QSC = nc.dram_tensor("QSC", [NB, 3, D, L], BF16, kind="Internal").ap()
        KTC = nc.dram_tensor("KTC", [NB, 3, D, L], BF16, kind="Internal").ap()
        KSC = nc.dram_tensor("KSC", [NB, 3, 2, D, L // 2], BF16, kind="Internal").ap()
        QN, MT, AO = ([nc.dram_tensor(f"{n}{b}", [L, w], F32, kind="Internal").ap() for b in range(NB)]
                      for n, w in (("QN", D), ("MT", H), ("AO", D)))
        IDX = nc.dram_tensor("IDX", [len(GROUPS), 8, 384], I32, kind="Internal").ap()
        QNr, AOr = ([v.rearrange("n (h d) -> (n h) d", d=DH) for v in vs] for vs in (QN, AO))
        MTr = [v.rearrange("n (h o) -> (n h) o", o=1) for v in MT]

        XT = sb("XT", [128, 8192])
        XH = XT[:, 0:4096].bitcast(F16).rearrange("p (k n) -> p k n", k=2)
        XL = XT[:, 4096:8192].bitcast(F16).rearrange("p (k n) -> p k n", k=2)
        VS = sb("VS", [128, NT, H, 2 * DH + 1], F16)
        KS = [sb(f"KS{i}", [128, 2, L // 2], BF16) for i in range(2)]
        QS = [sb(f"QS{i}", [128, L], BF16) for i in range(2)]
        KA = sb("KA", [128, L], BF16)
        AB = [sb(f"AB{i}", [128, 1024]) for i in range(3)]
        JK = [sb(f"JK{i}", [128, 1024], BF16) for i in range(2)]
        E = [sb(f"E{i}", [128, U]) for i in range(NE)]
        EH = [E[i][:].bitcast(BF16).rearrange("p (u w) -> p u w", w=2)[:, :, 1] for i in range(NE)]
        W2 = {n: sb("W_" + n, [128, 2, D]) for n in ("k", "o", "rT", "kT", "vT")}
        WH = {n: (sb(f"W{n}h", [128, 2, D], F16), sb(f"W{n}l", [128, 2, D], F16)) for n in ("k", "q", "v")}
        ident = sb("ident", [128, 128])
        identb = sb("identb", [128, 128], BF16)
        onesb = sb("onesb", [128, 128], BF16)
        trib = sb("trib", [128, 128], BF16)
        cols = sb("cols", [128, 16])
        bvb = sb("bvb", [128, D])
        bob = sb("bob", [128, D])
        zero = sb("zero", [128, D])
        tokc = sb("tokc", [128, NT], F16)
        halfc = sb("halfc", [128, 1])
        xpart = sb("xpart", [128, 2, 8])
        xbar = sb("xbar", [128, 2])
        SCR = sb("SCR", [128, 8704])
        kf, kr, kt = SCR[:, 0:1024], SCR[:, 1024:2048], SCR[:, 5632:6656]
        sp3 = [[SCR[:, 2048 + 512 * (3 * i + s):2560 + 512 * (3 * i + s)].bitcast(BF16) for s in range(3)]
               for i in range(2)]
        xin = [SCR[:, 5632 + 1024 * i:6656 + 1024 * i].rearrange("p (j c) -> p j c", j=4) for i in range(2)]
        qn = SCR[:, 7680:8704].rearrange("p (j c) -> p j c", j=8)
        OB = SCR[:, 0:2048].bitcast(F16).rearrange("p (a n) -> p a n", a=16)
        OA = SCR[:, 2048:4608].bitcast(F16).rearrange("p (a n) -> p a n", a=A_COLS)
        QG = SCR[:, 4608:4992].rearrange("p (k d) -> p k d", d=DH)
        QH = SCR[:, 4992:5376].rearrange("p (k d) -> p k d", d=DH)
        QST = SCR[:, 5376:6912].bitcast(BF16).rearrange("p (k d) -> p k d", d=128)
        EL = [SCR[:, 6912 + 154 * i:7066 + 154 * i].bitcast(F16)[:, 0:U] for i in range(NE)]
        fa = sb("fa", [128, NT * 8], F16)
        fb = sb("fb", [128, NT * 8], F16)
        SPr = sb("SPr", [128, NT, 8, 2])
        SS = [sb(f"S{g}", [128, NT, n]) for g, (_, _, n) in enumerate(GROUPS)]
        dif = sb("dif", [128, NT, 8])
        msk = sb("msk", [128, NT, 8], BF16)
        msk2 = sb("msk2", [128, NT, 8], BF16)
        msk3 = sb("msk3", [128, NT, 8], BF16)
        cand = sb("cand", [128, 8], I32)
        vbit = sb("vbit", [128, 8], I32)
        need = sb("need", [128, 8])
        slotf = dif
        sloti = sb("sloti", [128, NT, 8], I32)
        sla = sloti
        slb = sb("slb", [128, NT, 8], I32)
        hoff = sb("hoff", [A_COLS, 8, 16], I32)
        idw = sb("idw", [A_COLS, 8, 16], I32)
        idxs = [sb(f"idxs{i}", [128, 8, 3], I32) for i in range(2)]
        MG = sb("MG", [128, 24])
        MH = sb("MH", [128, 24])
        QT = [sb(f"QT{i}", [128, 320], BF16) for i in range(2)]
        OT = [sb(f"OT{i}", [2 * DH + 1, 384]) for i in range(2)]
        rec = sb("rec", [128, 3])
        osum = sb("osum", [128, 3, DH])
        OG = [sb(f"OG{i}", [128, 3, DH]) for i in range(2)]
        room = [0]

        def ff_tiles(count, w=D):
            tiles = [XT[:, room[0] + w * i:room[0] + w * (i + 1)] for i in range(count)]
            room[0] += w * count
            return tiles

        fx, fao, fh, fx1, fo, fr = ff_tiles(3), ff_tiles(3), ff_tiles(2), ff_tiles(4), ff_tiles(2), ff_tiles(2)
        faT, fm0, fm1, fk, fk2 = ([c.rearrange("p (k n) -> p k n", k=2) for c in ff_tiles(2)] for _ in range(5))
        fmp = ff_tiles(1)[0].rearrange("p (k n) -> p k n", k=2)
        x1T = [c.rearrange("p (k n) -> p k n", k=2) for c in ff_tiles(3, 258)]
        fst = sb("fst", [128, 2, 6])
        fmv = sb("fmv", [128, 4, 2])
        frs = sb("frs", [128, 4, 2])

        CP = ctx.enter_context(nc.psum_tensor("CP", [128, 2, 512], F32))
        BP = ctx.enter_context(nc.psum_tensor("BP", [128, 512], F32))
        PV = ctx.enter_context(nc.psum_tensor("PV", [128, 512], F32))
        DP = ctx.enter_context(nc.psum_tensor("DP", [128, 2, 1024], F32))
        C = Ring([CP[:, i, :] for i in range(2)])
        B = Ring([BP[:]])
        DR = Ring([DP[:, i, :] for i in range(2)])

        spent = [0.0]

        def charge(a, b):
            n = 1
            for w in b.shape[1:]:
                n *= w
            spent[0] += max(n, 64) * (4 if a.dtype == F32 else 1) / 2400.0

        def fill(ring, mms, *toks):
            s, slot, free = ring.take()
            pe.waits((free if free and isinstance(free[0], tuple) else (free or None,)) + toks)
            for n, (o, a, b, st, en) in enumerate(mms):
                charge(a, b)
                f = lambda e, o=o(slot), a=a, b=b, st=st, en=en: e.matmul(o, a, b, start=st, stop=en)
                if n == len(mms) - 1:
                    t = pe.do(f)
                else:
                    pe.quiet(f)
            return s, slot, t

        def turn(ring, trs, *toks):
            s, slot, free = ring.take()
            pe.waits((free if free and isinstance(free[0], tuple) else (free or None,)) + toks)
            for n, (o, a, i) in enumerate(trs):
                spent[0] += 128 / 2400.0
                f = lambda e, o=o(slot), a=a, i=i: e.transpose(o, a, i)
                if n == len(trs) - 1:
                    t = pe.do(f)
                else:
                    pe.quiet(f)
            return s, slot, t

        l_w = line("l_w")
        l_z = line("l_z")
        t_zero = pool.do(lambda e: e.memset(zero[:], 0.0))
        pool.do(lambda e: e.memset(ident[:], 0.0))
        pool.do(lambda e: e.memset(onesb[:], 1.0))
        t = pool.do(lambda e: e.memset(halfc[:], -0.5))
        pool.do(lambda e: e.affine_select(out=ident[:], in_=ident[:], compare_op=ALU.not_equal, fill=1.0, base=0,
                                          pattern=[[-1, 128]], channel_multiplier=1), t)
        t = pool.do(lambda e: e.affine_select(out=trib[:], in_=onesb[:], compare_op=ALU.is_ge, fill=0.0, base=0,
                                              pattern=[[1, 128]], channel_multiplier=-1))
        t_id = pool.do(lambda e: e.tensor_copy(identb[:], ident[:]), t)
        pool.do(lambda e: e.iota(tokc[:], pattern=[[128, NT]], base=-L // 2, channel_multiplier=1,
                                 allow_small_or_imprecise_dtypes=True))
        pool.do(lambda e: e.memset(MG[:], 0.0))
        for i in range(2):
            pool.do(lambda e, i=i: e.memset(OT[i][:], 1.0))
        t = pool.do(lambda e: e.memset(KA[96:128, :], 1.0), (pool.sem, pool.n))
        pool.waits([t])
        t_const = pool.do(lambda e: e.memset(VS[:, :, :, 2 * DH:2 * DH + 1], 1.0))

        def wload(dst, src):
            return l_w.dma(sp, lambda e: e.dma_start(dst, src))

        wraw = {"k": W2["k"][:], "q": QS[1][:, 0:1024].bitcast(F32).rearrange("p (k n) -> p k n", k=2),
                "v": QS[1][:, 1024:2048].bitcast(F32).rearrange("p (k n) -> p k n", k=2)}
        for d, w in ((wraw["k"], Wk), (wraw["q"], Wq), (wraw["v"], Wv), (W2["o"][:], Wo)):
            wload(d, w.rearrange("(k p) n -> p k n", p=128))
        raw = {"rT": (AB[0], W_r), "kT": (AB[1], W_k), "vT": (AB[2], W_v)}
        for n, (buf, w) in raw.items():
            wload(buf[:, 0:512].rearrange("p (k c) -> p k c", k=2), w.rearrange("(k p) c -> p k c", p=128))
        BQ, BK, MR, MK, SH, MR1, MK1, KB = (slice(2 * i, 2 * i + 2) for i in range(8))
        for c, v in ((BQ, bq), (BK, bk), (MR, mu_r), (MK, mu_k)):
            for k in range(2):
                wload(cols[:, c.start + k:c.start + k + 1], v[128 * k:128 * k + 128].unsqueeze(1))
        for d, v in ((bvb, bv), (bob, bo)):
            wload(d[:], v.partition_broadcast(128))
        t_w = l_w.all
        t_wh = {}
        for n, sc in (("k", WS / 2), ("q", WS), ("v", WS)):
            w, (wh, wl) = wraw[n], WH[n]
            t = pool.do(lambda e, w=w, sc=sc: e.tensor_scalar(w, w, sc, 0.0, ALU.mult, ALU.add), t_w)
            t = pool.do(lambda e, w=w, wh=wh: e.tensor_copy(wh[:], w), t)
            t_wh[n] = pool.do(lambda e, w=w, wh=wh, wl=wl: e.tensor_tensor(wl[:], w, wh[:], ALU.subtract), t)
        pool.do(lambda e: e.tensor_scalar(cols[:, BK], cols[:, BK], WS / 2, None, ALU.mult), t_w)
        pool.do(lambda e: e.tensor_scalar(cols[:, MR1], cols[:, MR], -1.0, 1.0, ALU.mult, ALU.add))
        t_cols = pool.do(lambda e: e.tensor_scalar(cols[:, MK1], cols[:, MK], -1.0, 1.0, ALU.mult, ALU.add))
        t_ffw = None
        for n, (buf, w) in raw.items():
            src = buf[:, 0:512].rearrange("p (k c) -> p k c", k=2)
            trs = [(lambda s, i=i, j=j: s[:, (2 * i + j) * 128:(2 * i + j + 1) * 128],
                    src[:, j, 128 * i:128 * i + 128], ident[:]) for i in range(2) for j in range(2)]
            s, slot, tp = turn(C, trs, t_w, t_id)
            t_ffw = C.free[s] = act.do(lambda e, n=n, slot=slot: e.activation(
                W2[n][:].rearrange("p k c -> p (k c)"), slot, ACT.Copy, scale=0.5 if n == "vT" else 1.0), tp)
        zs = zero[:].unsqueeze(1).broadcast_to([128, NT, D])
        for b in range(NB):
            l_z.dma(sp, lambda e, b=b: e.dma_start(AO[b].rearrange("(t p) c -> p t c", p=128), zs), t_zero)
            l_z.dma(sp, lambda e, b=b: e.dma_start(
                MT[b].rearrange("n h -> (n h)").rearrange("(p a c) -> p a c", p=128, a=2),
                zero[:].unsqueeze(1).broadcast_to([128, 2, D])), t_zero)

        l_x = [line(f"l_x{i}") for i in range(2)]
        l_s = [line(f"l_s{i}") for i in range(2)]
        l_q = [line(f"l_q{i}") for i in range(2)]
        t_xin = [None, None]
        t_kf = [None]
        t_sp = [0]
        ready = {}
        xt_free = [None]

        now = {"fast": True}

        def dup(e, o, v):
            return e.tensor_scalar(o, v, 1.0, 0.0, ALU.mult, ALU.add)

        def split(src, *src_t):
            i = t_sp[0] % 2
            t_sp[0] += 1
            hi, mid, lo = sp3[i]
            old = l_s[i].all
            fast = now["fast"]
            d = dve if fast else pool
            cp = (lambda o, v, *w: act.do(lambda e: e.copy(o, v), *w)) if fast else \
                 (lambda o, v, *w: pool.do(lambda e: dup(e, o, v), *w))
            t1 = cp(hi, src, old, *src_t)
            t2 = d.do(lambda e: e.tensor_tensor(kr, src, hi, ALU.subtract), t1, t_kf[0], *src_t)
            t3 = cp(mid, kr, t2)
            t4 = d.do(lambda e: e.tensor_tensor(lo, kr, mid, ALU.subtract), t3, old)
            t_kf[0] = t4
            return i, (t1, t3, t4)

        def parts(o, n, cs, ws, moving):
            mms = []
            for j, (xa, wi) in enumerate(((XH, 0), (XL, 0), (XH, 1))):
                for k in range(2):
                    xv, wv = xa[:, k, cs], WH[n][wi][:, k, ws]
                    a, b_ = (wv, xv) if moving else (xv, wv)
                    mms.append((o, a, b_, (j, k) == (0, 0), (j, k) == (2, 1)))
            return mms

        t_qn = [None]

        def project(b):
            xb = x[b]
            def load_x(c):
                i = c % 2
                l_x[i].dma(sp, lambda e: e.dma_start(
                    xin[i], xb[c * 512:(c + 1) * 512, :].rearrange("(j p) c -> p j c", p=128)), t_xin[i], t_kf[0])
            load_x(0)
            load_x(1)
            for _ in range(3):
                yield
            for c in range(8):
                i = c % 2
                t = l_x[i].all
                for k in range(2):
                    trs = [(lambda s, j=j: s[:, 128 * j:128 * j + 128], xin[i][:, j, 128 * k:128 * k + 128], ident[:])
                           for j in range(4)]
                    s, slot, tp = turn(C, trs, t, t_id)
                    t_xin[i] = tp
                    cs = slice(c * 512, (c + 1) * 512)
                    t_xt = act.do(lambda e, c=c, k=k, slot=slot, cs=cs: e.activation(
                        XH[:, k, cs], slot, ACT.Copy, accum_out=xpart[:, k, c:c + 1]), tp, xt_free[0])
                    t_xl = dve.do(lambda e, k=k, slot=slot, cs=cs: e.tensor_tensor(
                        XL[:, k, cs], slot, XH[:, k, cs], ALU.subtract), t_xt)
                    C.free[s] = (t_xt, t_xl)
                    yield
                if c < 6:
                    load_x(c + 2)
            t = dve.do(lambda e: e.reduce_sum(xbar[:], xpart[:], mybir.AxisListType.X), t_xt)
            t = dve.do(lambda e: e.tensor_scalar(xbar[:], xbar[:], 1.0 / L, None, ALU.mult), t)
            mms = [(lambda s, h=h: s[:, h:h + 1], W2["k"][:, k, 128 * h:128 * h + 128], xbar[:, k:k + 1], k == 0, k == 1)
                   for h in range(2) for k in range(2)]
            yield
            s, slot, tp = fill(B, mms, t, t_wh["k"])
            t = dve.do(lambda e, slot=slot: e.tensor_tensor(cols[:, KB], slot[:, 0:2], cols[:, BK], ALU.add), tp, t_cols)
            B.free[s] = t
            t_sh = dve.do(lambda e: e.tensor_tensor(cols[:, SH], cols[:, BK], cols[:, KB], ALU.subtract), t)
            yield
            for half in range(2):
                hs = slice(128 * half, 128 * half + 128)
                sh = cols[:, SH.start + half:SH.start + half + 1]
                bqc = cols[:, BQ.start + half:BQ.start + half + 1]

                def mms_of(n, c):
                    return parts(lambda s: s[:, 0:512], n, slice(c * 512, (c + 1) * 512), hs, True)
                for c in range(4):
                    w = (t_sh, t_kf[0], t_qn[0], t_xin[0])
                    s, slot, tp = fill(C, mms_of("k", c + 4), t_xt, t_xl, t_wh["k"])
                    t1 = C.free[s] = act.do(lambda e, slot=slot, sh=sh: e.activation(
                        kt[:, 512:1024], slot, ACT.Identity, bias=sh), tp, *w)
                    yield
                    s, slot, tp = fill(B, mms_of("k", c))
                    t2 = B.free[s] = dve.do(lambda e, slot=slot, sh=sh: e.tensor_scalar(
                        kt[:, 0:512], slot[:, 0:512], sh, None, ALU.add), tp, *w)
                    en = dve if now["fast"] else pool
                    t3 = en.do(lambda e: e.tensor_tensor(kf[:, 0:512], kt[:, 0:512], kt[:, 512:1024], ALU.add),
                               t1, t2, t_kf[0], t_qn[0])
                    t4 = en.do(lambda e: e.tensor_tensor(kf[:, 512:1024], kt[:, 0:512], kt[:, 512:1024], ALU.subtract))
                    for _ in range(3):
                        yield
                    i, ts = split(kf, t3, t4)
                    for m in range(3):
                        l_s[i].dma(sp, lambda e, m=m, i=i, c=c, hs=hs: e.dma_start(
                            KSC[b, m, :, hs, c * 512:(c + 1) * 512].rearrange("m p n -> p m n"),
                            sp3[i][m].rearrange("p (m n) -> p m n", m=2)), ts[m])
                    for _ in range(5):
                        yield
                    i, ts = split(kt, t1, t2)
                    for m in range(3):
                        l_s[i].dma(sp, lambda e, m=m, i=i, c=c, hs=hs: e.dma_start(
                            KTC[b, m, hs, :].rearrange("p (m n) -> p m n", m=2)[:, :, c * 512:(c + 1) * 512],
                            sp3[i][m].rearrange("p (m n) -> p m n", m=2)), ts[m])
                    for _ in range(5):
                        yield
                for c in range(4):
                    for j in range(2):
                        s, slot, tp = fill(C, mms_of("q", 2 * c + j), t_wh["q"])
                        t = C.free[s] = act.do(lambda e, slot=slot, bqc=bqc, j=j: e.activation(
                            kf[:, 512 * j:512 * j + 512], slot, ACT.Identity, bias=bqc, scale=1.0 / WS), tp, t_kf[0],
                            t_qn[0])
                        yield
                    i, ts = split(kf, t)
                    for m in range(3):
                        l_s[i].dma(sp, lambda e, m=m, i=i, c=c, hs=hs: e.dma_start(
                            QSC[b, m, hs, c * 1024:(c + 1) * 1024], sp3[i][m]), ts[m])
                    yield
                    yield
                    for j in range(2):
                        trs = [(lambda s, q=q: s[:, 128 * q:128 * q + 128],
                                kf[:, 128 * (4 * j + q):128 * (4 * j + q + 1)], ident[:]) for q in range(4)]
                        s, slot, tp = turn(C, trs, t)
                        t_qn[0] = tp
                        tq = C.free[s] = act.do(lambda e, slot=slot, j=j: e.copy(
                            qn[:, 4 * j:4 * j + 4, :].rearrange("p j c -> p (j c)"), slot), tp, l_q[0].all)
                        yield
                    l_q[0].dma(sp, lambda e, c=c, hs=hs: e.dma_start(
                        QN[b][c * 1024:(c + 1) * 1024, hs].rearrange("(j p) c -> p j c", p=128), qn), tq)
                    for _ in range(4):
                        yield
                ready[b, half] = (l_s[0].all, l_s[1].all)
            ready["v", b] = (l_q[0].all,)

        vs_free = [None]
        t_vs = {}

        def values(b):
            for t in range(NT):
                s, slot, tp = fill(C, parts(lambda s: s[:, 0:D], "v", slice(128 * t, 128 * t + 128), slice(0, D), False),
                                   t_wh["v"])
                sv = slot[:, 0:D].rearrange("p (h d) -> p h d", d=DH)
                ta = act.do(lambda e, sv=sv, t=t: e.mul(VS[:, t, :, 0:DH], sv, 1.0 / WS), tp, vs_free[0], t_const)
                tb = dve.do(lambda e, sv=sv, t=t: e.scalar_tensor_tensor(
                    out=VS[:, t, :, DH:2 * DH], in0=sv, scalar=1.0 / WS, in1=VS[:, t, :, 0:DH],
                    op0=ALU.mult, op1=ALU.subtract), ta, vs_free[0])
                C.free[s] = (ta, tb)
                yield
            t_vs[b] = (ta, tb)
            xt_free[0] = tp

        l_k = [line(f"l_k{i}") for i in range(2)]
        t_head = [None, None]
        t_ab = [None] * 3
        t_jk = [None] * 2
        kper = [0]

        def load_stack(ln, rows, w):
            for r, v in enumerate(rows):
                ln.dma(sp, lambda e, v=v: e.dma_start(*v), *w)

        def load_head(n):
            b, h = divmod(n, H)
            i = n % 2
            w = (t_head[i],) + ready[b, h // 8]
            hr = slice(16 * h, 16 * h + 16)
            load_stack(l_k[i], [(KS[i][16 * r:16 * r + 16, :, :], KSC[b, m, :, hr, :].rearrange("m p n -> p m n"))
                                for r, m in enumerate(KORD)], w)
            load_stack(l_k[i], [(QS[i][16 * r:16 * r + 16, :], QSC[b, m, hr, :]) for r, m in enumerate(QORD)], w)

        t_sp_free = [None]

        def here():
            return tuple((e.sem, e.n) for e in (pe, act, dve, pool) if e.n)

        def period(n, g, hl, t, u):
            i = n % 2
            k = kper[0]
            kper[0] += 1
            q = QS[i][0:96, 128 * t:128 * t + 128]
            ld = l_k[i].all
            ab, jk = AB[k % 3], JK[k % 2]
            for j in range(2):
                c0 = 1024 * u + 512 * j
                s, slot, tp = fill(C, [(lambda s: s, q, KS[i][0:96, 1, c0:c0 + 512], True, True)], ld)
                ta = C.free[s] = act.do(lambda e, slot=slot, j=j, ab=ab: e.activation(
                    ab[:, 512 * j:512 * j + 512], slot, ACT.Abs), tp, t_ab[k % 3], t_ffw)
            mms = [(lambda s, j=j: s[:, 512 * j:512 * j + 512], q,
                    KS[i][0:96, 0, 1024 * u + 512 * j:1024 * u + 512 * j + 512], True, True) for j in range(2)]
            s, slot, tp = fill(DR, mms)
            t_head[i] = tp
            w = t_sp_free[0] if (t, u, hl) == (0, 0, 0) else None
            td = dve.do(lambda e, slot=slot: e.tensor_tensor_reduce(
                out=jk[:], in0=slot, in1=ab[:], scale=1.0, scalar=-3.0e38, op0=ALU.add, op1=ALU.max,
                accum_out=SPr[:, t, hl, u:u + 1]), tp, ta, t_jk[k % 2], w)
            DR.free[s] = t_ab[k % 3] = t_jk[k % 2] = td
            return td

        l_m = line("l_m")
        l_i = line("l_i")
        l_g = line("l_g")
        l_a = line("l_a")
        l_o = [line(f"l_o{i}") for i in range(2)]
        st = {"ka": None, "qt": [None, None], "pv": None, "e": [None] * NE, "ne": 0, "na": 0,
              "ot": [None, None], "qst": None, "og": None, "idx": [(), ()], "ix": None}

        def prefix(m, n, tm):
            mms = [(lambda s: s[:, 0:NT * n], trib[:], m, True, False)]
            for t in range(NT - 1):
                r = m[:, t:t + 1, :].broadcast_to([128, NT - 1 - t, n])
                mms.append((lambda s, t=t: s[:, (t + 1) * n:NT * n], onesb[:], r, False, t == NT - 2))
            return fill(B, mms, tm, t_id)

        def capture(g, t_spars):
            n = GROUPS[g][2]
            sg = SS[g][:]
            t = dve.do(lambda e: e.scalar_tensor_tensor(
                out=sg, in0=SPr[:, :, 0:n, 0], scalar=0.0, in1=SPr[:, :, 0:n, 1], op0=ALU.max, op1=ALU.max),
                t_spars)
            t_sp_free[0] = t
            return t

        def select(g, t_s, slow):
            b, h0, n = GROUPS[g]
            edge = here()
            sg = SS[g][:]
            m1, m2, m3 = (m[:].rearrange("p t h -> p (t h)")[:, 0:NT * n].rearrange("p (t h) -> p t h", h=n)
                          for m in (msk, msk2, msk3))
            cd = cand[:, 0:n]
            cf = cand[:].bitcast(F32)[:, 0:n].unsqueeze(1).broadcast_to([128, NT, n])
            t = t_s
            MTb = MT[b][:, h0:h0 + n].rearrange("(t p) h -> p t h", p=128)
            t_m = l_m.dma(sp, lambda e: e.dma_start(MTb, sg), t, l_z.all)
            t = dve.do(lambda e: e.memset(cd, 1 << 30))
            tp_free = None
            for bit in range(30, -1, -1):
                t1 = dve.do(lambda e: e.tensor_tensor(m1, sg, cf, ALU.is_ge), t, t_s, tp_free, *edge)
                if slow:
                    for w in (16, 8, 4):
                        t1 = pool.do(lambda e, w=w: e.tensor_tensor(m1[:, 0:w, :], m1[:, 0:w, :], m1[:, w:2 * w, :],
                                                                    ALU.add), t1)
                    for _ in range(4):
                        yield "wait"
                w = 4 if slow else NT
                s, slot, tp = fill(B, [(lambda s: s[:, 0:n], onesb[:], m1[:, j, :], j == 0, j == w - 1)
                                        for j in range(w)], t1)
                tp_free = tp
                t2 = B.free[s] = dve.do(lambda e, slot=slot, bit=bit: e.tensor_scalar(
                    vbit[:, 0:n], slot[:, 0:n], float(U), float(1 << bit), ALU.is_lt, ALU.mult), tp)
                t = dve.do(lambda e, bit=bit: e.scalar_tensor_tensor(
                    out=cd, in0=vbit[:, 0:n], scalar=(1 << bit) >> 1, in1=cd,
                    op0=ALU.bitwise_xor, op1=ALU.bitwise_xor), t2)
            t1 = dve.do(lambda e: e.tensor_tensor(m1, sg, cf, ALU.is_gt), t, tp_free)
            t2 = dve.do(lambda e: e.tensor_tensor(m2, sg, cf, ALU.is_equal))
            for _ in range(3 * slow):
                yield "wait"
            s, slot, tp = fill(B, [(lambda s: s[:, 0:n], onesb[:], m1[:, j, :], j == 0, j == NT - 1)
                                    for j in range(NT)], t1)
            t = B.free[s] = dve.do(lambda e, slot=slot: e.tensor_scalar(need[:, 0:n], slot[:, 0:n], -1.0, float(U),
                                                              ALU.mult, ALU.add), tp)
            s, slot, tp = prefix(m2, n, t2)
            nb = need[:, 0:n].unsqueeze(1).broadcast_to([128, NT, n])
            t = B.free[s] = dve.do(lambda e, slot=slot: e.tensor_tensor(
                m3, slot[:, 0:NT * n].rearrange("p (t h) -> p t h", h=n), nb, ALU.is_le), tp, t)
            t = dve.do(lambda e: e.tensor_tensor(m3, m3, m2, ALU.mult), t)
            t = dve.do(lambda e: e.tensor_tensor(m3, m3, m1, ALU.add), t)
            for _ in range(2 * slow):
                yield "wait"
            s, slot, tp = prefix(m3, n, t)
            sf, si = (q[:].rearrange("p t h -> p (t h)")[:, 0:NT * n] for q in (slotf, sloti))
            ai, bi = (q[:].rearrange("p t h -> p (t h)")[:, 0:NT * n] for q in (sla, slb))
            m3f = msk3[:].rearrange("p t h -> p (t h)")[:, 0:NT * n]
            t = B.free[s] = dve.do(lambda e, slot=slot: e.tensor_tensor(sf, slot[:, 0:NT * n], m3f, ALU.mult), tp)
            if slow:
                yield "wait"
            t = dve.do(lambda e: e.tensor_scalar(si, sf, -1.0, None, ALU.add), t)
            t2 = dve.do(lambda e: e.tensor_scalar(bi, si, 15, None, ALU.bitwise_and), t)
            t1 = dve.do(lambda e: e.tensor_scalar(ai, si, 4, None, ALU.arith_shift_right), t2)
            t1 = pool.do(lambda e: dup(e, fa[:, 0:NT * n], ai), t1)
            t2 = pool.do(lambda e: dup(e, fb[:, 0:NT * n], bi), t2)
            tk = tokc[:].unsqueeze(2).broadcast_to([128, NT, n])
            for _ in range(2 * slow):
                yield "wait"
            t_m2 = []
            for j in range(16):
                t = dve.do(lambda e, j=j: e.tensor_scalar(OB[:, j, 0:NT * n], fb[:, 0:NT * n], float(j), None,
                                                          ALU.is_equal), t2, *edge)
                v = OB[:, j, 0:NT * n].rearrange("p (t h) -> p t h", h=n)
                t_b = pool.do(lambda e, v=v: e.tensor_tensor(v, v, tk, ALU.mult), t)
                if slow and j % 4 == 3:
                    yield "wait"
            for j in range(A_COLS):
                t_a = dve.do(lambda e, j=j: e.tensor_scalar(OA[:, j, 0:NT * n], fa[:, 0:NT * n], float(j), None,
                                                            ALU.is_equal), t1)
                if slow and j % 4 == 3:
                    yield "wait"
            for _ in range(3 * slow):
                yield "wait"
            t_ho = pool.do(lambda e: e.iota(hoff[:], pattern=[[1, 8], [0, 16]], base=16 * (L // 2) + h0,
                                            channel_multiplier=0), *edge)
            for h in range(n):
                mms = [(lambda s: s[0:A_COLS, 0:16], OA[:, :, n * j + h], OB[:, :, n * j + h], j == 0, j == NT - 1)
                       for j in range(NT)]
                s, slot, tp = fill(B, mms, t_a, t_b)
                t = B.free[s] = dve.do(lambda e, slot=slot, h=h: e.scalar_tensor_tensor(
                    out=idw[:, h, :], in0=slot[0:A_COLS, 0:16], scalar=16.0, in1=hoff[:, h, :],
                    op0=ALU.mult, op1=ALU.add), tp, l_i.all, t_ho)
                if slow:
                    yield "wait"
            st["ix"] = tp
            t = l_i.dma(sp, lambda e: e.dma_start(
                IDX[g, 0:n, 0:16 * A_COLS].rearrange("h (a b) -> a h b", b=16), idw[:, 0:n, :]), t)
            ix = idxs[g % 2]
            tw = t
            for c, (a0, w) in enumerate(CH):
                t = l_i.dma(sp, lambda e, c=c, a0=a0, w=w: e.dma_start(
                    ix[0:w, 0:n, c], IDX[g, 0:n, a0:a0 + w].rearrange("h s -> s h")), tw, *st["idx"][g % 2])
            sel[g] = (t, t_m)

        sel = {}

        def attend(g, slow):
            b, h0, n = GROUPS[g]
            t, t_m = sel[g]
            ix = idxs[g % 2]
            if g == 0:
                edge = here()
                pool.do(lambda e: e.memset(QG, 0.0), *edge)
                pool.do(lambda e: e.memset(QST, 0.0))
            for _ in range(6 * slow):
                yield "wait"
            ixf = ix[:].rearrange("p h c -> p (h c)")
            for h in range(n):
                for c, (_, w) in enumerate(CH):
                    k = 3 * h + c
                    l_g.dma(pool, lambda e, k=k, w=w: e.indirect_dma_start(
                        out=QG[0:w, k, :], out_offset=None, in_=QNr[b],
                        in_offset=bass.IndirectOffsetOnAxis(ap=ixf[0:w, k:k + 1], axis=0)),
                        t, t_m, st["qst"], (pool.sem, pool.n), *ready["v", b])
                    l_g.dma(pool, lambda e, k=k, w=w: e.indirect_dma_start(
                        out=MG[0:w, k:k + 1], out_offset=None, in_=MTr[b],
                        in_offset=bass.IndirectOffsetOnAxis(ap=ixf[0:w, k:k + 1], axis=0)))
                    if slow:
                        yield "wait"
            for _ in range(3 * slow):
                yield "wait"
            hc = 3 * n
            q, r = QG[:, 0:hc, :], QH[:, 0:hc, :]
            z = [QST[:, 0:hc, 16 * k:16 * k + 16] for k in range(6)]
            t = pool.do(lambda e: dup(e, z[0], q), l_g.all, st["qst"])
            pool.do(lambda e: dup(e, z[1], z[0]), t)
            pool.do(lambda e: dup(e, z[3], z[0]))
            t = pool.do(lambda e: e.tensor_tensor(r, q, z[0], ALU.subtract))
            t = pool.do(lambda e: dup(e, z[2], r), t)
            pool.do(lambda e: dup(e, z[5], z[2]), t)
            pool.do(lambda e: e.tensor_tensor(z[4], r, z[2], ALU.subtract))
            mz = [QST[:, 0:hc, 96 + k] for k in range(3)]
            m, mr = MG[:, 0:hc], MH[:, 0:hc]
            t = pool.do(lambda e: e.tensor_scalar(mr, m, -0.5, 0.0, ALU.mult, ALU.add))
            t = pool.do(lambda e: e.tensor_copy(mz[0], mr), t)
            t = pool.do(lambda e: e.tensor_tensor(mr, mr, mz[0], ALU.subtract), t)
            t = pool.do(lambda e: e.tensor_copy(mz[1], mr), t)
            t_q = pool.do(lambda e: e.tensor_tensor(mz[2], mr, mz[1], ALU.subtract), t)

            for _ in range(4 * slow):
                yield

            pend = []
            tail = not slow

            def flush(lim, h):
                while len(pend) > lim:
                    j, tile, te = pend.pop(0)
                    first, last = tile == 0, tile == 2 * 16 - 1
                    pe.quiet(lambda e, j=j, tile=tile, first=first: e.matmul(
                        PV[0:2 * DH + 1, 0:U], VS[:, tile, h, :], EH[j], start=first, stop=False),
                        te, st["pv"] if first else None, *t_vs[b])
                    spent[0] += 2 * U / 2400.0
                    tp = pe.do(lambda e, j=j, tile=tile, last=last: e.matmul(
                        PV[0:2 * DH + 1, 0:U], VS[:, tile, h, :], EL[j], start=False, stop=last))
                    st["e"][j] = tp
                    st["pvt"] = tp

            def load_ka(h):
                hr = slice(16 * h, 16 * h + 16)
                load_stack(l_a, [(KA[16 * r:16 * r + 16, :], KTC[b, m, hr, :]) for r, m in enumerate(KORD)],
                           (st["ka"], t_const) + ready[b, h // 8])

            for hl in range(n):
                h = h0 + hl
                i = h % 2
                load_ka(h)
                trs = [(lambda s, a=a, w=w: s.bitcast(BF16)[:, a:a + w], QST[0:w, 3 * hl + c, :],
                        identb[0:w, 0:w]) for c, (a, w) in enumerate(CH[:2])]
                trs.append((lambda s: s.bitcast(BF16)[:, 256:256 + CH[2][1] + 1], QST[0:52, 3 * hl + 2, :],
                            identb[0:52, 0:52]))
                s, slot, tp = turn(C, trs, t_q, t_id)
                st["qst"] = tp
                t2 = C.free[s] = act.do(lambda e, slot=slot, i=i: e.copy(QT[i][:, 0:U], slot.bitcast(BF16)[:, 0:U]),
                                        tp, st["qt"][i])
                ld = l_a.all
                for _ in range(4 * slow):
                    yield
                for kc in range(NT):
                    s, slot, tp = fill(B, [(lambda s: s[:, 0:U], KA[0:99, 128 * kc:128 * kc + 128],
                                            QT[i][0:99, 0:U], True, True)], t2, ld)
                    j = st["ne"] % NE
                    st["ne"] += 1
                    te = B.free[s] = act.do(lambda e, slot=slot, j=j: e.activation(
                        E[j][:], slot[:, 0:U], ACT.Exp, scale=2 * SCALE / WS), tp, st["e"][j])
                    te = (dve if tail else pool).do(lambda e, j=j: e.tensor_tensor(
                        EL[j], E[j][:], EH[j], ALU.subtract), te, st["e"][j])
                    pend.append((j, kc, te))
                    flush(PVLAG, h)
                    if slow:
                        yield
                st["ka"] = st["qt"][i] = tp
                flush(0, h)
                if slow:
                    yield
                t = st["pv"] = act.do(lambda e, i=i: e.copy(OT[i][:, 0:U], PV[0:2 * DH + 1, 0:U]), st["pvt"],
                                      st["ot"][i], t_const)
                for _ in range(2 * slow):
                    yield
                trs = [(lambda s, c=c: s[:, 64 * c:64 * c + 2 * DH + 1], OT[i][:, 128 * c:128 * c + 128],
                        ident[0:2 * DH + 1, 0:2 * DH + 1]) for c in range(3)]
                s, slot, tp = turn(B, trs, t)
                st["ot"][i] = tp
                sv = slot[:, 0:192].rearrange("p (c d) -> p c d", c=3)
                t1 = dve.do(lambda e, sv=sv: e.reciprocal(rec[:], sv[:, :, 2 * DH]), tp, st.get("rec"))
                t = dve.do(lambda e, sv=sv: e.tensor_copy(osum[:], sv[:, :, 0:DH]), st.get("rec"))
                t = dve.do(lambda e, sv=sv: e.tensor_tensor(osum[:], osum[:], sv[:, :, DH:2 * DH], ALU.add), t)
                B.free[s] = t
                t = dve.do(lambda e, i=i: e.tensor_tensor(
                    OG[i][:], osum[:], rec[:].unsqueeze(2).broadcast_to([128, 3, DH]), ALU.mult),
                    t, t1, l_o[i].all)
                st["rec"] = t
                bv3 = bvb[:, DH * h:DH * h + DH].unsqueeze(1).broadcast_to([128, 3, DH])
                t = pool.do(lambda e, i=i, bv3=bv3: e.tensor_tensor(OG[i][:], OG[i][:], bv3, ALU.add), t, t_w)
                for c, (_, w) in enumerate(CH):
                    l_o[i].dma(pool, lambda e, i=i, c=c, w=w, k=3 * hl + c: e.indirect_dma_start(
                        out=AOr[b], out_offset=bass.IndirectOffsetOnAxis(ap=ixf[0:w, k:k + 1], axis=0),
                        in_=OG[i][0:w, c, :], in_offset=None), t, l_z.all)
                if slow:
                    yield
            st["scat"] = st["idx"][g % 2] = (l_o[0].all, l_o[1].all)
            vs_free[0] = st["pvt"]

        l_f = [line(f"l_f{i}") for i in range(3)]
        l_out = [line(f"l_out{i}") for i in range(2)]
        def feed(b, scat, slow):
            tail = not slow
            xb = x[b]
            edge = here()
            for e in (act, dve, pool, sp):
                e.waits(edge)
            pool.do(lambda e: e.memset(x1T[0][:, :, 0:1], 0.0))
            T = {}

            def g(*keys):
                return tuple(T.get(k) for k in keys)

            def rstd(t, q):
                v, r = fmv[:, q, :], frs[:, q, :]
                t = pool.do(lambda e: e.tensor_scalar(r[:, 0:1], v[:, 1:2], EPS, None, ALU.add), t, *g(("n", q)))
                t = pool.do(lambda e: e.tensor_tensor(r[:, 0:1], r[:, 0:1], halfc[:], ALU.pow), t)
                if not tail:
                    t = pool.do(lambda e: e.tensor_tensor(r[:, 1:2], v[:, 0:1], r[:, 0:1], ALU.mult), t)
                    t = pool.do(lambda e: e.tensor_scalar(r[:, 1:2], r[:, 1:2], -1.0, 0.0, ALU.mult, ALU.add), t)
                return t

            def norm(src, dst, q, *toks):
                v, r = fmv[:, q, :], frs[:, q, :]
                if tail:
                    t = dve.do(lambda e: e.tensor_scalar(dst, src, v[:, 0:1], r[:, 0:1], ALU.subtract, ALU.mult), *toks)
                else:
                    t = pool.do(lambda e: e.tensor_scalar(dst, src, r[:, 0:1], r[:, 1:2], ALU.mult, ALU.add), *toks)
                T["n", q] = t
                return t

            def stats(src, q, *toks):
                i = q % 2
                t = dve.do(lambda e: e.bn_stats(fst[:, i, :], src), *toks, *g(("st", i)))
                t = T["st", i] = dve.do(lambda e: e.bn_aggr(fmv[:, q, :], fst[:, i, :]), t, *g(("n", q)))
                return t

            def f0(t):
                i = t % 3
                l_f[i].dma(sp, lambda e: e.dma_start(fx[i], xb[128 * t:128 * t + 128, :]),
                           *scat, *g(("y", t - 3), ("T0", t - 3), ("xb", t - 3)))
                T["ld", t] = l_f[i].dma(sp, lambda e: e.dma_start(fao[i], AO[b][128 * t:128 * t + 128, :]))

            def f1(t):
                i, j = t % 3, t % 2
                s, slot, tp = turn(C, [(lambda s, k=k: s[:, 128 * k:128 * k + 128],
                                        fao[i][:, 128 * k:128 * k + 128], ident[:]) for k in range(2)], *g(("ld", t)))
                T["T0", t] = tp
                T["aT", t] = C.free[s] = act.do(lambda e: e.copy(
                    faT[j].rearrange("p k n -> p (k n)"), slot[:, 0:256]), tp, *g(("yp", t - 2)))
                T["xb", t] = pool.do(lambda e: e.tensor_tensor(fx[i], fx[i], bob[:], ALU.add), *g(("ld", t)), t_w)

            def f2(t):
                i, j = t % 3, t % 2
                s, slot, tp = fill(B, [(lambda s: s[:, 0:D], faT[j][:, k, :], W2["o"][:, k, :], k == 0, k == 1)
                                        for k in range(2)], t_w, *g(("aT", t)))
                T["yp", t] = tp
                t1 = T["y", t] = B.free[s] = dve.do(lambda e: e.tensor_tensor(
                    fh[j], slot[:, 0:D], fx[i], ALU.add), tp, *g(("xb", t), ("x1", t - 2)))
                T["s1", t] = rstd(stats(fh[j], j, t1), j)

            def f3(t):
                j = t % 2
                T["x1", t] = norm(fh[j], fx1[t % 4], j, *g(("s1", t), ("o2", t - 4), ("T1", t - 4)))

            def f4(t):
                i = t % 3
                s, slot, tp = turn(C, [(lambda s, k=k: s[:, 128 * k:128 * k + 128],
                                        fx1[t % 4][:, 128 * k:128 * k + 128], ident[:]) for k in range(2)],
                                   *g(("x1", t)))
                T["T1", t] = tp
                sv = slot[:, 0:256].rearrange("p (k n) -> p k n", k=2)
                ta = act.do(lambda e: e.copy(x1T[i][:, :, 1:129], sv), tp, *g(("mx", t - 3), ("mx", t - 2)))
                T["x1T", t] = C.free[s] = act.do(lambda e: e.copy(x1T[(t + 1) % 3][:, :, 0:1], sv[:, :, 127:128]))

            def f5(t):
                i, j = t % 3, t % 2
                cur, prv = x1T[i][:, :, 1:129], x1T[i][:, :, 0:128]
                for m, (ca, cb) in enumerate(((MR, MR1), (MK, MK1))):
                    fm = (fm0, fm1)[m][j]
                    w = g(("x1T", t), ("mx", t - 1), ("r", t - 2), ("k", t - 2))
                    for k in range(2):
                        tq = pool.do(lambda e, k=k, cb=cb: e.tensor_scalar(
                            fmp[:, k, :], prv[:, k, :], cols[:, cb.start + k:cb.start + k + 1], 0.0, ALU.mult, ALU.add),
                            *w, t_cols, *g("fmp"))
                        if tail:
                            T["mx", t] = T["fmp"] = dve.do(lambda e, k=k, ca=ca, fm=fm: e.scalar_tensor_tensor(
                                out=fm[:, k, :], in0=cur[:, k, :], scalar=cols[:, ca.start + k:ca.start + k + 1],
                                in1=fmp[:, k, :], op0=ALU.mult, op1=ALU.add), tq)
                        else:
                            tq = pool.do(lambda e, k=k, ca=ca, fm=fm: e.tensor_scalar(
                                fm[:, k, :], cur[:, k, :], cols[:, ca.start + k:ca.start + k + 1], 0.0, ALU.mult,
                                ALU.add))
                    if not tail:
                        T["mx", t] = T["fmp"] = pool.do(lambda e, fm=fm: e.tensor_tensor(fm, fm, fmp, ALU.add), tq)

            def f6(t):
                j = t % 2
                s, slot, tp = fill(C, [(lambda s: s[:, 0:D], fm0[j][:, k, :], W2["rT"][:, k, :], k == 0, k == 1)
                                       for k in range(2)], t_ffw, *g(("mx", t)))
                T["r", t] = tp
                T["th", t] = C.free[s] = act.do(lambda e: e.activation(fr[j], slot[:, 0:D], ACT.Tanh, scale=0.5),
                                                tp, *g(("o1", t - 2)))
                s2, slot2, tp = fill(C, [(lambda s, m=m: s[:, 128 * m:128 * m + 128],
                                          W2["kT"][:, k, 128 * m:128 * m + 128], fm1[j][:, k, :], k == 0, k == 1)
                                         for m in range(2) for k in range(2)])
                T["k", t] = tp
                tk = C.free[s2] = act.do(lambda e: e.activation(
                    fk[j].rearrange("p k n -> p (k n)"), slot2[:, 0:256], ACT.Relu), tp, *g(("sq", t - 2)))
                T["sq", t] = pool.do(lambda e: e.tensor_tensor(fk2[j], fk[j], fk[j], ALU.mult), tk, *g(("v", t - 2)))

            def f7(t):
                j = t % 2
                s, slot, tp = fill(B, [(lambda s: s[:, 0:D], fk2[j][:, k, :], W2["vT"][:, k, :], k == 0, k == 1)
                                        for k in range(2)], *g(("sq", t)))
                T["v", t] = tp
                t1 = T["o1", t] = B.free[s] = dve.do(lambda e: e.scalar_tensor_tensor(
                    out=fo[j], in0=fr[j], scalar=1.0, in1=slot[:, 0:D], op0=ALU.add, op1=ALU.mult),
                    tp, l_out[j].all, *g(("th", t), ("o3", t - 2)))
                T["o2", t] = (dve if tail else pool).do(lambda e: e.tensor_tensor(
                    fo[j], fo[j], fx1[t % 4], ALU.add), t1)

            def f8(t):
                j = t % 2
                T["s2", t] = rstd(stats(fo[j], 2 + j, *g(("o2", t))), 2 + j)

            def f9(t):
                j = t % 2
                tn = T["o3", t] = norm(fo[j], fo[j], 2 + j, *g(("s2", t)))
                l_out[j].dma(sp, lambda e: e.dma_start(out[b, 128 * t:128 * t + 128, :], fo[j]), tn)

            stages = [f0, f1, f2, f3, f4, f5, f6, f7, f8, f9]
            for k in range(NT + len(stages) - 1):
                for n, f in reversed(list(enumerate(stages))):
                    if 0 <= k - n < NT:
                        f(k - n)
                        yield

        def drain(job):
            for _ in job:
                pass

        lanes = {"s": [], "a": [], "b": []}

        def step(lane):
            q = lanes[lane]
            while q:
                try:
                    return next(q[0]) or "work"
                except StopIteration:
                    q.pop(0)
            return None

        def until(key):
            while key not in ready:
                assert step("b")

        done = {}

        def select_job(g):
            while (1, 1) not in ready:
                yield "wait"
            yield from select(g, t_cap[g], 1 if g + 1 < len(GROUPS) else 0)

        def attend_job(g):
            while g not in sel:
                yield "wait"
            yield from attend(g, 1 if g + 1 < len(GROUPS) else 0)
            done[g] = st["scat"]

        def rest():
            while 1 not in done:
                yield "wait"
            yield from values(1)
            done["v"] = True
            yield from feed(0, done[1], 1)

        def wait_values():
            while "v" not in done:
                yield "wait"

        t_cap = {}
        lanes["b"] += [project(0)]
        until((0, 0))
        now["fast"] = False
        lanes["b"] += [values(0), project(1), rest()]
        load_head(0)
        n = 0
        credit = 0.0

        def background():
            step("s")
            s0 = spent[0]
            for lane in ("a", "b", "b"):
                if spent[0] - s0 < credit and step(lane) != "work":
                    pass
            return spent[0] - s0

        for g, (b, h0, cnt) in enumerate(GROUPS):
            for hl in range(cnt):
                if n + 1 < NB * H:
                    until(((n + 1) // H, (n + 1) % H // 8))
                    load_head(n + 1)
                for t in range(NT):
                    for u in range(2):
                        td = period(n, g, hl, t, u)
                        credit = min(credit + BUDGET, 4 * BUDGET)
                        credit -= background()
                n += 1
            t_cap[g] = capture(g, td)
            lanes["s"].append(select_job(g))
            if g == 2:
                lanes["a"].append(wait_values())
            lanes["a"].append(attend_job(g))
        while step("s") or step("a") or step("b"):
            pass
        for _ in feed(1, st["scat"], 0):
            pass
        for ln in (l_w, l_z, l_m, l_i, l_g, *l_s, *l_q, l_a, *l_o, *l_f, *l_out):
            sp.waits([ln.all])

        ctx.enter_context(nc.allow_non_contiguous_dma(reason="columns, indices and maxima are small"))
        block = ctx.enter_context(nc.Block())
        block.tensor(pe.run)
        block.scalar(act.run)
        block.vector(dve.run)
        block.gpsimd(pool.run)
        block.sync(sp.run)


_INS = ['L0_attn_x', 'L0_attn_Wq', 'L0_attn_bq', 'L0_attn_Wk', 'L0_attn_bk', 'L0_attn_Wv', 'L0_attn_bv',
        'L0_attn_Wo', 'L0_attn_bo', 'L0_ffn_W_r', 'L0_ffn_W_k', 'L0_ffn_W_v', 'L0_ffn_mu_r', 'L0_ffn_mu_k']


def kernel(**inputs):
    import numpy as np
    import concourse.bacc as bacc
    from concourse.bass_utils import run_bass_kernel_spmd as run

    nc = bacc.Bacc("TRN2", target_bir_lowering=False, num_devices=1)
    arrays, args = {}, []
    for name in _INS:
        a = np.ascontiguousarray(inputs[name])
        arrays[f"in_{name}"] = a
        args.append(nc.dram_tensor(f"in_{name}", a.shape, F32, kind="ExternalInput").ap())
    out = nc.dram_tensor("out_0", (NB, L, D), F32, kind="ExternalOutput").ap()
    attention_rwkv(nc, *args, out)
    r = run(nc, [arrays], core_ids=[0])
    return r.results[0]["out_0"]
```

```python
from contextlib import ExitStack

import concourse.bass as bass
from concourse import mybir

F32 = mybir.dt.float32
BF16 = mybir.dt.bfloat16
F16 = mybir.dt.float16
I32 = mybir.dt.int32
ALU = mybir.AluOpType
ACT = mybir.ActivationFunctionType

NB, L, D, H, DH = 2, 4096, 256, 16, 16
NT = L // 128
U = max(1, min(512, int(0.6 * 512)))
SCALE = 0.25
EPS = 1e-5
A_COLS = (U + 15) // 16
CH = [(0, 128), (128, 128), (256, U - 256)]
KORD = [0, 1, 0, 2, 0, 1]
QORD = [0, 0, 1, 0, 2, 1]
GROUPS = [(0, 0, 6), (0, 6, 6), (0, 12, 4), (1, 0, 6), (1, 6, 6), (1, 12, 4)]
G1 = 3
BUDGET = 0.55
WS = 64.0
NE = 10
PVLAG = 6


class Engine:

    def __init__(self, sem):
        self.sem, self.n, self.q, self.seen = sem, 0, [], {}

    def waits(self, toks):
        for t in toks:
            if t is None:
                continue
            s, v = t
            if self.seen.get(id(s), 0) < v:
                self.seen[id(s)] = v
                self.q.append(("w", s, v))

    def do(self, f, *toks):
        self.waits(toks)
        self.n += 1
        self.q.append(("i", f, self.sem, 1))
        return (self.sem, self.n)

    def quiet(self, f, *toks):
        self.waits(toks)
        self.q.append(("i", f, None, 0))

    def run(self, e):
        for item in self.q:
            if item[0] == "w":
                e.wait_ge(item[1], item[2])
            else:
                r = item[1](e)
                if item[2] is not None:
                    r.then_inc(item[2], item[3])


class Line:

    def __init__(self, sem):
        self.sem, self.n = sem, 0

    def dma(self, eng, f, *toks):
        eng.waits(toks)
        self.n += 16
        eng.q.append(("i", f, self.sem, 16))
        return (self.sem, self.n)

    @property
    def all(self):
        return (self.sem, self.n) if self.n else None


class Ring:

    def __init__(self, slots):
        self.slots, self.free, self.i = slots, [()] * len(slots), 0

    def take(self):
        s = self.i % len(self.slots)
        self.i += 1
        return s, self.slots[s], self.free[s]


def attention_rwkv(nc, x, Wq, bq, Wk, bk, Wv, bv, Wo, bo, W_r, W_k, W_v, mu_r, mu_k, out):
    ctx = ExitStack()
    with ctx:
        def sb(name, shape, dt=F32):
            return ctx.enter_context(nc.sbuf_tensor(name, shape, dt))

        def sem(name):
            return ctx.enter_context(nc.semaphore(name))

        def line(name):
            return Line(sem(name))

        pe, act, dve, pool, sp = (Engine(sem("s_" + n)) for n in ("pe", "act", "dve", "pool", "sp"))

        QSC = nc.dram_tensor("QSC", [NB, 3, D, L], BF16, kind="Internal").ap()
        KTC = nc.dram_tensor("KTC", [NB, 3, D, L], BF16, kind="Internal").ap()
        KSC = nc.dram_tensor("KSC", [NB, 3, 2, D, L // 2], BF16, kind="Internal").ap()
        QN, AO = ([nc.dram_tensor(f"{n}{b}", [L, w], F32, kind="Internal").ap() for b in range(NB)]
                  for n, w in (("QN", H * (DH + 1)), ("AO", D)))
        IDX = nc.dram_tensor("IDX", [len(GROUPS), 8, 384], I32, kind="Internal").ap()
        QNr, AOr = ([v.rearrange("n (h d) -> (n h) d", d=d) for v in vs] for vs, d in ((QN, DH + 1), (AO, DH)))

        XT = sb("XT", [128, 8192])
        XH = XT[:, 0:4096].bitcast(F16).rearrange("p (k n) -> p k n", k=2)
        XL = XT[:, 4096:8192].bitcast(F16).rearrange("p (k n) -> p k n", k=2)
        VS = sb("VS", [128, NT, H, 2 * DH + 1], F16)
        KS = [sb(f"KS{i}", [128, 2, L // 2], BF16) for i in range(2)]
        QS = [sb(f"QS{i}", [128, L], BF16) for i in range(2)]
        KA = sb("KA", [128, L], BF16)
        AB = [sb(f"AB{i}", [128, 1024]) for i in range(3)]
        JK = [sb(f"JK{i}", [128, 1024], BF16) for i in range(2)]
        E = [sb(f"E{i}", [128, U]) for i in range(NE)]
        EH = [E[i][:].bitcast(BF16).rearrange("p (u w) -> p u w", w=2)[:, :, 1] for i in range(NE)]
        W2 = {n: sb("W_" + n, [128, 2, D]) for n in ("k", "o", "rT", "kT", "vT")}
        WH = {n: (sb(f"W{n}h", [128, 2, D], F16), sb(f"W{n}l", [128, 2, D], F16)) for n in ("k", "q", "v")}
        ident = sb("ident", [128, 128])
        identb = sb("identb", [128, 128], BF16)
        onesb = sb("onesb", [128, 128], BF16)
        trib = sb("trib", [128, 128], BF16)
        cols = sb("cols", [128, 16])
        bvb = sb("bvb", [128, D])
        bob = sb("bob", [128, D])
        zero = sb("zero", [128, D])
        tokc = sb("tokc", [128, NT], F16)
        halfc = sb("halfc", [128, 1])
        xpart = sb("xpart", [128, 2, 8])
        xbar = sb("xbar", [128, 2])
        SCR = sb("SCR", [128, 8768])
        kf, kr, kt = SCR[:, 0:1024], SCR[:, 1024:2048], SCR[:, 5632:6656]
        sp3 = [[SCR[:, 2048 + 512 * (3 * i + s):2560 + 512 * (3 * i + s)].bitcast(BF16) for s in range(3)]
               for i in range(2)]
        xin = [SCR[:, 5632 + 1024 * i:6656 + 1024 * i].rearrange("p (j c) -> p j c", j=4) for i in range(2)]
        qn = SCR[:, 7680:8768].rearrange("p (j h d) -> p j h d", j=8, d=DH + 1)
        OB = SCR[:, 0:2048].bitcast(F16).rearrange("p (a n) -> p a n", a=16)
        OA = SCR[:, 2048:4608].bitcast(F16).rearrange("p (a n) -> p a n", a=A_COLS)
        QG = SCR[:, 4608:5016].rearrange("p (k d) -> p k d", d=DH + 1)
        QH = SCR[:, 5016:5400].rearrange("p (k d) -> p k d", d=DH)
        QST = SCR[:, 5400:6936].bitcast(BF16).rearrange("p (k d) -> p k d", d=128)
        EL = [SCR[:, 6936 + 154 * i:7090 + 154 * i].bitcast(F16)[:, 0:U] for i in range(NE)]
        fa = sb("fa", [128, NT * 8], F16)
        fb = sb("fb", [128, NT * 8], F16)
        SPr = sb("SPr", [128, NT, 8, 2])
        SS = [sb(f"S{g}", [128, NT, n]) for g, (_, _, n) in enumerate(GROUPS)]
        dif = sb("dif", [128, NT, 8])
        msk = sb("msk", [128, NT, 8], BF16)
        msk2 = sb("msk2", [128, NT, 8], BF16)
        msk3 = sb("msk3", [128, NT, 8], BF16)
        cand = sb("cand", [128, 8], I32)
        vbit = sb("vbit", [128, 8], I32)
        need = sb("need", [128, 8])
        cntb = sb("cntb", [128, 8])
        slotf = dif
        sloti = sb("sloti", [128, NT, 8], I32)
        sla = sloti
        slb = sb("slb", [128, NT, 8], I32)
        hoff = sb("hoff", [A_COLS, 8, 16], I32)
        idw = sb("idw", [A_COLS, 8, 16], I32)
        idxs = [sb(f"idxs{i}", [128, 8, 3], I32) for i in range(len(GROUPS))]
        MH = sb("MH", [128, 24])
        QT = [sb(f"QT{i}", [128, 320], BF16) for i in range(2)]
        OT = [sb(f"OT{i}", [2 * DH + 1, 384]) for i in range(2)]
        rec = sb("rec", [128, 3])
        osum = sb("osum", [128, 3, DH])
        OG = [sb(f"OG{i}", [128, 3, DH]) for i in range(2)]
        room = [0]

        def ff_tiles(count, w=D):
            tiles = [XT[:, room[0] + w * i:room[0] + w * (i + 1)] for i in range(count)]
            room[0] += w * count
            return tiles

        fx, fao, fh, fx1, fr = ff_tiles(3), ff_tiles(3), ff_tiles(2), ff_tiles(4), ff_tiles(2)
        faT, fm0, fm1, fk, fk2 = ([c.rearrange("p (k n) -> p k n", k=2) for c in ff_tiles(2)] for _ in range(5))
        fmp = [c.rearrange("p (k n) -> p k n", k=2) for c in ff_tiles(2)]
        x1T = [c.rearrange("p (k n) -> p k n", k=2) for c in ff_tiles(3, 258)]
        fo = [*ff_tiles(2), W2["k"][:, 0, :], W2["k"][:, 1, :]]
        fst = sb("fst", [128, 2, 6])
        fmv = sb("fmv", [128, 4, 2])
        frs = sb("frs", [128, 4, 2])

        CP = ctx.enter_context(nc.psum_tensor("CP", [128, 2, 512], F32))
        BP = ctx.enter_context(nc.psum_tensor("BP", [128, 512], F32))
        PV = ctx.enter_context(nc.psum_tensor("PV", [128, 512], F32))
        DP = ctx.enter_context(nc.psum_tensor("DP", [128, 2, 1024], F32))
        C = Ring([CP[:, i, :] for i in range(2)])
        B = Ring([BP[:], PV[:]])
        DR = Ring([DP[:, i, :] for i in range(2)])

        spent = [0.0]

        def charge(a, b):
            n = 1
            for w in b.shape[1:]:
                n *= w
            spent[0] += max(n, 64) * (4 if a.dtype == F32 else 1) / 2400.0

        def fill(ring, mms, *toks):
            s, slot, free = ring.take()
            pe.waits((free if free and isinstance(free[0], tuple) else (free or None,)) + toks)
            for n, (o, a, b, first, last) in enumerate(mms):
                charge(a, b)
                f = lambda e, o=o(slot), a=a, b=b, first=first, last=last: e.matmul(
                    o, a, b, start=first, stop=last)
                if n == len(mms) - 1:
                    t = pe.do(f)
                else:
                    pe.quiet(f)
            return s, slot, t

        def fill_slowly(ring, mms, *toks):
            s, slot, free = ring.take()
            st["open"] = True
            pe.waits((free if free and isinstance(free[0], tuple) else (free or None,)) + toks)
            for n, (o, a, b, first, last) in enumerate(mms):
                charge(a, b)
                f = lambda e, o=o(slot), a=a, b=b, first=first, last=last: e.matmul(
                    o, a, b, start=first, stop=last)
                if n == len(mms) - 1:
                    t = pe.do(f)
                    st["open"] = False
                else:
                    pe.quiet(f)
                    if now["main"] and (n % 2 or (a.dtype == F32 and len(mms) == 2)):
                        yield
            return s, slot, t

        def turn(ring, trs, *toks):
            s, slot, free = ring.take()
            pe.waits((free if free and isinstance(free[0], tuple) else (free or None,)) + toks)
            for n, (o, a, i) in enumerate(trs):
                spent[0] += 128 / 2400.0
                f = lambda e, o=o(slot), a=a, i=i: e.transpose(o, a, i)
                if n == len(trs) - 1:
                    t = pe.do(f)
                else:
                    pe.quiet(f)
            return s, slot, t

        l_w = line("l_w")
        l_z = line("l_z")
        t_zero = pool.do(lambda e: e.memset(zero[:], 0.0))
        pool.do(lambda e: e.memset(ident[:], 0.0))
        pool.do(lambda e: e.memset(onesb[:], 1.0))
        t = pool.do(lambda e: e.memset(halfc[:], -0.5))
        pool.do(lambda e: e.affine_select(out=ident[:], in_=ident[:], compare_op=ALU.not_equal, fill=1.0, base=0,
                                          pattern=[[-1, 128]], channel_multiplier=1), t)
        t = pool.do(lambda e: e.affine_select(out=trib[:], in_=onesb[:], compare_op=ALU.is_ge, fill=0.0, base=0,
                                              pattern=[[1, 128]], channel_multiplier=-1))
        t_id = pool.do(lambda e: e.tensor_copy(identb[:], ident[:]), t)
        pool.do(lambda e: e.iota(tokc[:], pattern=[[128, NT]], base=-L // 2, channel_multiplier=1,
                                 allow_small_or_imprecise_dtypes=True))
        for i in range(2):
            pool.do(lambda e, i=i: e.memset(OT[i][:], 1.0))
        t = pool.do(lambda e: e.memset(KA[96:128, :], 1.0), (pool.sem, pool.n))
        pool.waits([t])
        t_const = pool.do(lambda e: e.memset(VS[:, :, :, 2 * DH:2 * DH + 1], 1.0))

        def wload(dst, src):
            return l_w.dma(sp, lambda e: e.dma_start(dst, src))

        wraw = {"k": W2["k"][:], "q": QS[1][:, 0:1024].bitcast(F32).rearrange("p (k n) -> p k n", k=2),
                "v": QS[1][:, 1024:2048].bitcast(F32).rearrange("p (k n) -> p k n", k=2)}
        for d, w in ((wraw["k"], Wk), (wraw["q"], Wq), (wraw["v"], Wv), (W2["o"][:], Wo)):
            wload(d, w.rearrange("(k p) n -> p k n", p=128))
        raw = {"rT": (AB[0], W_r), "kT": (AB[1], W_k), "vT": (AB[2], W_v)}
        for n, (buf, w) in raw.items():
            wload(buf[:, 0:512].rearrange("p (k c) -> p k c", k=2), w.rearrange("(k p) c -> p k c", p=128))
        BQ, BK, MR, MK, SH, MR1, MK1, KB = (slice(2 * i, 2 * i + 2) for i in range(8))
        for c, v in ((BQ, bq), (BK, bk), (MR, mu_r), (MK, mu_k)):
            for k in range(2):
                wload(cols[:, c.start + k:c.start + k + 1], v[128 * k:128 * k + 128].unsqueeze(1))
        for d, v in ((bvb, bv), (bob, bo)):
            wload(d[:], v.partition_broadcast(128))
        t_w = l_w.all
        t_wh = {}
        for n, sc in (("k", WS / 2), ("q", WS), ("v", WS)):
            w, (wh, wl) = wraw[n], WH[n]
            t = pool.do(lambda e, w=w, sc=sc: e.tensor_scalar(w, w, sc, 0.0, ALU.mult, ALU.add), t_w)
            t = pool.do(lambda e, w=w, wh=wh: e.tensor_copy(wh[:], w), t)
            t_wh[n] = pool.do(lambda e, w=w, wh=wh, wl=wl: e.tensor_tensor(wl[:], w, wh[:], ALU.subtract), t)
        pool.do(lambda e: e.tensor_scalar(cols[:, BK], cols[:, BK], WS / 2, None, ALU.mult), t_w)
        pool.do(lambda e: e.tensor_scalar(cols[:, MR1], cols[:, MR], -1.0, 1.0, ALU.mult, ALU.add))
        t_cols = pool.do(lambda e: e.tensor_scalar(cols[:, MK1], cols[:, MK], -1.0, 1.0, ALU.mult, ALU.add))
        t_ffw = None
        for n, (buf, w) in raw.items():
            src = buf[:, 0:512].rearrange("p (k c) -> p k c", k=2)
            trs = [(lambda s, i=i, j=j: s[:, (2 * i + j) * 128:(2 * i + j + 1) * 128],
                    src[:, j, 128 * i:128 * i + 128], ident[:]) for i in range(2) for j in range(2)]
            s, slot, tp = turn(C, trs, t_w, t_id)
            t_ffw = C.free[s] = act.do(lambda e, n=n, slot=slot: e.activation(
                W2[n][:].rearrange("p k c -> p (k c)"), slot, ACT.Copy, scale=0.5 if n == "vT" else 1.0), tp)
        zs = zero[:].unsqueeze(1).broadcast_to([128, NT, D])
        for b in range(NB):
            l_z.dma(sp, lambda e, b=b: e.dma_start(AO[b].rearrange("(t p) c -> p t c", p=128), zs), t_zero)

        l_x = [line(f"l_x{i}") for i in range(2)]
        l_s = [line(f"l_s{i}") for i in range(2)]
        l_q = [line(f"l_q{i}") for i in range(2)]
        t_xin = [None, None]
        t_kf = [None]
        t_sp = [0]
        ready = {}
        xt_free = [None]

        now = {"fast": True, "main": True}

        def dup(e, o, v):
            return e.tensor_scalar(o, v, 1.0, 0.0, ALU.mult, ALU.add)

        def split(src, *src_t):
            i = t_sp[0] % 2
            t_sp[0] += 1
            hi, mid, lo = sp3[i]
            old = l_s[i].all
            fast = now["fast"]
            d = dve if fast else pool
            cp = (lambda o, v, *w: act.do(lambda e: e.copy(o, v), *w)) if fast else \
                 (lambda o, v, *w: pool.do(lambda e: dup(e, o, v), *w))
            t1 = cp(hi, src, old, *src_t)
            t2 = d.do(lambda e: e.tensor_tensor(kr, src, hi, ALU.subtract), t1, t_kf[0], *src_t)
            t3 = cp(mid, kr, t2)
            t4 = d.do(lambda e: e.tensor_tensor(lo, kr, mid, ALU.subtract), t3, old)
            t_kf[0] = t4
            return i, (t1, t3, t4)

        def parts(o, n, cs, ws, moving):
            mms = []
            for j, (xa, wi) in enumerate(((XH, 0), (XL, 0), (XH, 1))):
                for k in range(2):
                    xv, wv = xa[:, k, cs], WH[n][wi][:, k, ws]
                    a, b_ = (wv, xv) if moving else (xv, wv)
                    mms.append((o, a, b_, (j, k) == (0, 0), (j, k) == (2, 1)))
            return mms

        t_qn = [None]

        def project(b):
            xb = x[b]
            def load_x(c):
                i = c % 2
                l_x[i].dma(sp, lambda e: e.dma_start(
                    xin[i], xb[c * 512:(c + 1) * 512, :].rearrange("(j p) c -> p j c", p=128)), t_xin[i], t_kf[0])
            load_x(0)
            load_x(1)
            t_qz = pool.do(lambda e: e.memset(qn[:, :, :, DH:DH + 1], 0.0), l_q[0].all, t_xin[0], *(
                [(pool.sem, pool.n)] if pool.n else []))
            for _ in range(3):
                yield
            for c in range(8):
                i = c % 2
                t = l_x[i].all
                for k in range(2):
                    trs = [(lambda s, j=j: s[:, 128 * j:128 * j + 128], xin[i][:, j, 128 * k:128 * k + 128], ident[:])
                           for j in range(4)]
                    s, slot, tp = turn(C, trs, t, t_id)
                    t_xin[i] = tp
                    cs = slice(c * 512, (c + 1) * 512)
                    t_xt = act.do(lambda e, c=c, k=k, slot=slot, cs=cs: e.activation(
                        XH[:, k, cs], slot, ACT.Copy, accum_out=xpart[:, k, c:c + 1]), tp, xt_free[0])
                    t_xl = dve.do(lambda e, k=k, slot=slot, cs=cs: e.tensor_tensor(
                        XL[:, k, cs], slot, XH[:, k, cs], ALU.subtract), t_xt)
                    C.free[s] = (t_xt, t_xl)
                    yield
                if c < 6:
                    load_x(c + 2)
            t = dve.do(lambda e: e.reduce_sum(xbar[:], xpart[:], mybir.AxisListType.X), t_xt)
            t = dve.do(lambda e: e.tensor_scalar(xbar[:], xbar[:], 1.0 / L, None, ALU.mult), t)
            mms = [(lambda s, h=h: s[:, h:h + 1], W2["k"][:, k, 128 * h:128 * h + 128], xbar[:, k:k + 1], k == 0, k == 1)
                   for h in range(2) for k in range(2)]
            yield
            s, slot, tp = fill(B, mms, t, t_wh["k"])
            t = dve.do(lambda e, slot=slot: e.tensor_tensor(cols[:, KB], slot[:, 0:2], cols[:, BK], ALU.add), tp, t_cols)
            B.free[s] = t
            t_sh = dve.do(lambda e: e.tensor_tensor(cols[:, SH], cols[:, BK], cols[:, KB], ALU.subtract), t)
            yield
            for half in range(2):
                hs = slice(128 * half, 128 * half + 128)
                sh = cols[:, SH.start + half:SH.start + half + 1]
                bqc = cols[:, BQ.start + half:BQ.start + half + 1]

                def mms_of(n, c):
                    return parts(lambda s: s[:, 0:512], n, slice(c * 512, (c + 1) * 512), hs, True)
                for c in range(4):
                    w = (t_sh, t_kf[0], t_qn[0], t_xin[0])
                    s, slot, tp = yield from fill_slowly(B, mms_of("k", c + 4), t_xt, t_xl, t_wh["k"])
                    t1 = B.free[s] = act.do(lambda e, slot=slot, sh=sh: e.activation(
                        kt[:, 512:1024], slot, ACT.Identity, bias=sh), tp, *w)
                    yield
                    s, slot, tp = yield from fill_slowly(B, mms_of("k", c))
                    t2 = B.free[s] = dve.do(lambda e, slot=slot, sh=sh: e.tensor_scalar(
                        kt[:, 0:512], slot[:, 0:512], sh, None, ALU.add), tp, *w)
                    en = dve if now["fast"] else pool
                    t3 = en.do(lambda e: e.tensor_tensor(kf[:, 0:512], kt[:, 0:512], kt[:, 512:1024], ALU.add),
                               t1, t2, t_kf[0], t_qn[0])
                    t4 = en.do(lambda e: e.tensor_tensor(kf[:, 512:1024], kt[:, 0:512], kt[:, 512:1024], ALU.subtract))
                    yield
                    i, ts = split(kf, t3, t4)
                    for m in range(3):
                        l_s[i].dma(sp, lambda e, m=m, i=i, c=c, hs=hs: e.dma_start(
                            KSC[b, m, :, hs, c * 512:(c + 1) * 512].rearrange("m p n -> p m n"),
                            sp3[i][m].rearrange("p (m n) -> p m n", m=2)), ts[m])
                    for _ in range(5):
                        yield
                    i, ts = split(kt, t1, t2)
                    for m in range(3):
                        l_s[i].dma(sp, lambda e, m=m, i=i, c=c, hs=hs: e.dma_start(
                            KTC[b, m, hs, :].rearrange("p (m n) -> p m n", m=2)[:, :, c * 512:(c + 1) * 512],
                            sp3[i][m].rearrange("p (m n) -> p m n", m=2)), ts[m])
                    for _ in range(5):
                        yield
                for c in range(4):
                    for j in range(2):
                        s, slot, tp = yield from fill_slowly(B, mms_of("q", 2 * c + j), t_wh["q"])
                        t = B.free[s] = act.do(lambda e, slot=slot, bqc=bqc, j=j: e.activation(
                            kf[:, 512 * j:512 * j + 512], slot, ACT.Identity, bias=bqc, scale=1.0 / WS), tp, t_kf[0],
                            t_qn[0])
                        yield
                    i, ts = split(kf, t)
                    for m in range(3):
                        l_s[i].dma(sp, lambda e, m=m, i=i, c=c, hs=hs: e.dma_start(
                            QSC[b, m, hs, c * 1024:(c + 1) * 1024], sp3[i][m]), ts[m])
                    yield
                    yield
                    for j in range(2):
                        trs = [(lambda s, q=q: s[:, 128 * q:128 * q + 128],
                                kf[:, 128 * (4 * j + q):128 * (4 * j + q + 1)], ident[:]) for q in range(4)]
                        s, slot, tp = turn(B, trs, t)
                        t_qn[0] = tp
                        tq = B.free[s] = act.do(lambda e, slot=slot, j=j: e.copy(
                            qn[:, 4 * j:4 * j + 4, :, 0:DH], slot.rearrange("p (j h d) -> p j h d", j=4, d=DH)), tp,
                            l_q[0].all, t_qz)
                        yield
                    l_q[0].dma(sp, lambda e, c=c, half=half: e.dma_start(
                        QN[b][c * 1024:(c + 1) * 1024, 136 * half:136 * half + 136].rearrange("(j p) c -> p j c", p=128),
                        qn.rearrange("p j h d -> p j (h d)")), tq)
                    for _ in range(4):
                        yield
                ready[b, half] = (l_s[0].all, l_s[1].all)
            ready["v", b] = (l_q[0].all,)

        vs_free = [None]
        t_vs = {}

        def values(b):
            for t in range(NT):
                s, slot, tp = fill(B, parts(lambda s: s[:, 0:D], "v", slice(128 * t, 128 * t + 128), slice(0, D), False),
                                   t_wh["v"])
                sv = slot[:, 0:D].rearrange("p (h d) -> p h d", d=DH)
                ta = act.do(lambda e, sv=sv, t=t: e.mul(VS[:, t, :, 0:DH], sv, 1.0 / WS), tp, vs_free[0], t_const)
                tb = dve.do(lambda e, sv=sv, t=t: e.scalar_tensor_tensor(
                    out=VS[:, t, :, DH:2 * DH], in0=sv, scalar=1.0 / WS, in1=VS[:, t, :, 0:DH],
                    op0=ALU.mult, op1=ALU.subtract), ta, vs_free[0])
                B.free[s] = (ta, tb)
                yield
            t_vs[b] = (ta, tb)
            xt_free[0] = tp

        l_k = [line(f"l_k{i}") for i in range(2)]
        t_head = [None, None]
        t_ab = [None] * 3
        t_jk = [None] * 2
        kper = [0]

        def load_stack(ln, rows, w):
            for r, v in enumerate(rows):
                ln.dma(sp, lambda e, v=v: e.dma_start(*v), *w)

        def load_head(n):
            b, h = divmod(n, H)
            i = n % 2
            w = (t_head[i],) + ready[b, h // 8]
            hr = slice(16 * h, 16 * h + 16)
            load_stack(l_k[i], [(KS[i][16 * r:16 * r + 16, :, :], KSC[b, m, :, hr, :].rearrange("m p n -> p m n"))
                                for r, m in enumerate(KORD)], w)
            load_stack(l_k[i], [(QS[i][16 * r:16 * r + 16, :], QSC[b, m, hr, :]) for r, m in enumerate(QORD)], w)

        t_sp_free = [None]

        def here():
            return tuple((e.sem, e.n) for e in (pe, act, dve, pool) if e.n)

        def period(n, g, hl, t, u):
            i = n % 2
            k = kper[0]
            kper[0] += 1
            q = QS[i][0:96, 128 * t:128 * t + 128]
            ld = l_k[i].all
            ab, jk = AB[k % 3], JK[k % 2]
            for j in range(2):
                c0 = 1024 * u + 512 * j
                s, slot, tp = fill(C, [(lambda s: s, q, KS[i][0:96, 1, c0:c0 + 512], True, True)], ld)
                ta = C.free[s] = act.do(lambda e, slot=slot, j=j, ab=ab: e.activation(
                    ab[:, 512 * j:512 * j + 512], slot, ACT.Abs), tp, t_ab[k % 3], t_ffw)
            mms = [(lambda s, j=j: s[:, 512 * j:512 * j + 512], q,
                    KS[i][0:96, 0, 1024 * u + 512 * j:1024 * u + 512 * j + 512], True, True) for j in range(2)]
            s, slot, tp = fill(DR, mms)
            t_head[i] = tp
            w = t_sp_free[0] if (t, u, hl) == (0, 0, 0) else None
            td = dve.do(lambda e, slot=slot: e.tensor_tensor_reduce(
                out=jk[:], in0=slot, in1=ab[:], scale=1.0, scalar=-3.0e38, op0=ALU.add, op1=ALU.max,
                accum_out=SPr[:, t, hl, u:u + 1]), tp, ta, t_jk[k % 2], w)
            DR.free[s] = t_ab[k % 3] = t_jk[k % 2] = td
            return td

        l_m = line("l_m")
        l_i = line("l_i")
        l_g = line("l_g")
        l_a = line("l_a")
        l_o = [line(f"l_o{i}") for i in range(2)]
        st = {"ka": None, "qt": [None, None], "pv": (), "lent": True, "open": False, "e": [None] * NE, "ne": 0,
              "ot": [None, None], "qst": None, "og": None, "ix": None}

        def prefix(m, n, tm):
            mms = [(lambda s: s[:, 0:NT * n], trib[:], m, True, False)]
            for t in range(NT - 1):
                r = m[:, t:t + 1, :].broadcast_to([128, NT - 1 - t, n])
                mms.append((lambda s, t=t: s[:, (t + 1) * n:NT * n], onesb[:], r, False, t == NT - 2))
            return fill(B, mms, tm, t_id)

        def capture(g, t_spars):
            n = GROUPS[g][2]
            sg = SS[g][:]
            t = dve.do(lambda e: e.scalar_tensor_tensor(
                out=sg, in0=SPr[:, :, 0:n, 0], scalar=0.0, in1=SPr[:, :, 0:n, 1], op0=ALU.max, op1=ALU.max),
                t_spars)
            t_sp_free[0] = t
            return t

        def select(g, t_s):
            b, h0, n = GROUPS[g]
            edge = here()
            sg = SS[g][:]
            m1, m2, m3 = (m[:].rearrange("p t h -> p (t h)")[:, 0:NT * n].rearrange("p (t h) -> p t h", h=n)
                          for m in (msk, msk2, msk3))
            cd = cand[:, 0:n]
            cf = cand[:].bitcast(F32)[:, 0:n].unsqueeze(1).broadcast_to([128, NT, n])
            t = t_s
            for h in range(n):
                c0 = (h0 + h) * (DH + 1) + DH
                t_m = l_m.dma(sp, lambda e, h=h, c0=c0: e.dma_start(
                    QN[b][:, c0:c0 + 1].rearrange("(t p) o -> p t o", p=128), sg[:, :, h:h + 1]), t, *ready["v", b])
            t = dve.do(lambda e: e.memset(cd, 1 << 30))
            tp_free = None
            for bit in range(30, -1, -1):
                t1 = dve.do(lambda e: e.tensor_tensor(m1, sg, cf, ALU.is_ge), t, t_s, tp_free, *edge)
                for w in (16, 8, 4):
                    t1 = (pool if now["main"] else dve).do(lambda e, w=w: e.tensor_tensor(m1[:, 0:w, :], m1[:, 0:w, :], m1[:, w:2 * w, :],
                                                                ALU.add), t1)
                for _ in range(5 if now["main"] else 2):
                    yield "wait"
                w = 4
                s, slot, tp = fill(B, [(lambda s: s[:, 0:n], onesb[:], m1[:, j, :], j == 0, j == w - 1)
                                        for j in range(w)], t1)
                tp_free = tp
                if now["main"] and g > 0:
                    tp = B.free[s] = act.do(lambda e, slot=slot: e.copy(cntb[:, 0:n], slot[:, 0:n]), tp, t)
                    yield "wait"
                    t2 = dve.do(lambda e, bit=bit: e.tensor_scalar(
                        vbit[:, 0:n], cntb[:, 0:n], float(U), float(1 << bit), ALU.is_lt, ALU.mult), tp)
                else:
                    t2 = B.free[s] = dve.do(lambda e, slot=slot, bit=bit: e.tensor_scalar(
                        vbit[:, 0:n], slot[:, 0:n], float(U), float(1 << bit), ALU.is_lt, ALU.mult), tp)
                t = dve.do(lambda e, bit=bit: e.scalar_tensor_tensor(
                    out=cd, in0=vbit[:, 0:n], scalar=(1 << bit) >> 1, in1=cd,
                    op0=ALU.bitwise_xor, op1=ALU.bitwise_xor), t2)
            t1 = dve.do(lambda e: e.tensor_tensor(m1, sg, cf, ALU.is_gt), t, tp_free)
            t2 = dve.do(lambda e: e.tensor_tensor(m2, sg, cf, ALU.is_equal))
            for _ in range(3):
                yield "wait"
            s, slot, tp = fill(B, [(lambda s: s[:, 0:n], onesb[:], m1[:, j, :], j == 0, j == NT - 1)
                                    for j in range(NT)], t1)
            t = B.free[s] = dve.do(lambda e, slot=slot: e.tensor_scalar(need[:, 0:n], slot[:, 0:n], -1.0, float(U),
                                                              ALU.mult, ALU.add), tp)
            yield "wait"
            s, slot, tp = prefix(m2, n, t2)
            nb = need[:, 0:n].unsqueeze(1).broadcast_to([128, NT, n])
            t = B.free[s] = dve.do(lambda e, slot=slot: e.tensor_tensor(
                m3, slot[:, 0:NT * n].rearrange("p (t h) -> p t h", h=n), nb, ALU.is_le), tp, t)
            t = dve.do(lambda e: e.tensor_tensor(m3, m3, m2, ALU.mult), t)
            t = dve.do(lambda e: e.tensor_tensor(m3, m3, m1, ALU.add), t)
            for _ in range(2):
                yield "wait"
            s, slot, tp = prefix(m3, n, t)
            sf, si = (q[:].rearrange("p t h -> p (t h)")[:, 0:NT * n] for q in (slotf, sloti))
            ai, bi = (q[:].rearrange("p t h -> p (t h)")[:, 0:NT * n] for q in (sla, slb))
            m3f = msk3[:].rearrange("p t h -> p (t h)")[:, 0:NT * n]
            t = B.free[s] = dve.do(lambda e, slot=slot: e.tensor_tensor(sf, slot[:, 0:NT * n], m3f, ALU.mult), tp)
            yield "wait"
            t = dve.do(lambda e: e.tensor_scalar(si, sf, -1.0, None, ALU.add), t)
            t2 = dve.do(lambda e: e.tensor_scalar(bi, si, 15, None, ALU.bitwise_and), t)
            t1 = dve.do(lambda e: e.tensor_scalar(ai, si, 4, None, ALU.arith_shift_right), t2)
            t1 = pool.do(lambda e: dup(e, fa[:, 0:NT * n], ai), t1)
            t2 = pool.do(lambda e: dup(e, fb[:, 0:NT * n], bi), t2)
            tk = tokc[:].unsqueeze(2).broadcast_to([128, NT, n])
            for _ in range(2):
                yield "wait"
            t_m2 = []
            for j in range(16):
                t = dve.do(lambda e, j=j: e.tensor_scalar(OB[:, j, 0:NT * n], fb[:, 0:NT * n], float(j), None,
                                                          ALU.is_equal), t2, *edge)
                v = OB[:, j, 0:NT * n].rearrange("p (t h) -> p t h", h=n)
                t_b = pool.do(lambda e, v=v: e.tensor_tensor(v, v, tk, ALU.mult), t)
                if j % 4 == 3:
                    yield "wait"
            for j in range(A_COLS):
                t_a = dve.do(lambda e, j=j: e.tensor_scalar(OA[:, j, 0:NT * n], fa[:, 0:NT * n], float(j), None,
                                                            ALU.is_equal), t1)
                if j % 4 == 3:
                    yield "wait"
            for _ in range(3):
                yield "wait"
            t_ho = pool.do(lambda e: e.iota(hoff[:], pattern=[[1, 8], [0, 16]], base=16 * (L // 2) + h0,
                                            channel_multiplier=0), *edge)
            for h in range(n):
                mms = [(lambda s: s[0:A_COLS, 0:16], OA[:, :, n * j + h], OB[:, :, n * j + h], j == 0, j == NT - 1)
                       for j in range(NT)]
                s, slot, tp = fill(B, mms, t_a, t_b)
                t = B.free[s] = dve.do(lambda e, slot=slot, h=h: e.scalar_tensor_tensor(
                    out=idw[:, h, :], in0=slot[0:A_COLS, 0:16], scalar=16.0, in1=hoff[:, h, :],
                    op0=ALU.mult, op1=ALU.add), tp, l_i.all, t_ho)
                yield "wait"
            st["ix"] = tp
            t = l_i.dma(sp, lambda e: e.dma_start(
                IDX[g, 0:n, 0:16 * A_COLS].rearrange("h (a b) -> a h b", b=16), idw[:, 0:n, :]), t)
            ix = idxs[g]
            tw = t
            for c, (a0, w) in enumerate(CH):
                t = l_i.dma(sp, lambda e, c=c, a0=a0, w=w: e.dma_start(
                    ix[0:w, 0:n, c], IDX[g, 0:n, a0:a0 + w].rearrange("h s -> s h")), tw)
            sel[g] = (t, t_m)

        sel = {}

        def attend(g):
            b, h0, n = GROUPS[g]
            t, t_m = sel[g]
            ix = idxs[g]
            st["lent"] = False
            B.slots.pop(1)
            f = B.free.pop(1)
            st["pv"] = f if not f or isinstance(f[0], tuple) else (f,)
            if g == 0:
                edge = here()
                pool.do(lambda e: e.memset(QG, 0.0), *edge)
                pool.do(lambda e: e.memset(QST, 0.0))
            for _ in range(6):
                yield "wait"
            ixf = ix[:].rearrange("p h c -> p (h c)")

            def gather(ha, hb):
                for h in range(ha, hb):
                    for c, (_, w) in enumerate(CH):
                        k = 3 * h + c
                        l_g.dma(pool, lambda e, k=k, w=w: e.indirect_dma_start(
                            out=QG[0:w, k, :], out_offset=None, in_=QNr[b],
                            in_offset=bass.IndirectOffsetOnAxis(ap=ixf[0:w, k:k + 1], axis=0)),
                            t, t_m, st["qst"], (pool.sem, pool.n), *ready["v", b])
                        yield "wait"

            def arrange(ha, hb):
                a = slice(3 * ha, 3 * hb)
                q, r = QG[:, a, 0:DH], QH[:, a, :]
                z = [QST[:, a, 16 * k:16 * k + 16] for k in range(6)]
                t = pool.do(lambda e: dup(e, z[0], q), l_g.all, st["qst"])
                pool.do(lambda e: dup(e, z[1], z[0]), t)
                pool.do(lambda e: dup(e, z[3], z[0]))
                t = pool.do(lambda e: e.tensor_tensor(r, q, z[0], ALU.subtract))
                t = pool.do(lambda e: dup(e, z[2], r), t)
                pool.do(lambda e: dup(e, z[5], z[2]), t)
                pool.do(lambda e: e.tensor_tensor(z[4], r, z[2], ALU.subtract))
                mz = [QST[:, a, 96 + k] for k in range(3)]
                m, mr = QG[:, a, DH], MH[:, a]
                t = pool.do(lambda e: e.tensor_scalar(mr, m, -0.5, 0.0, ALU.mult, ALU.add))
                t = pool.do(lambda e: e.tensor_copy(mz[0], mr), t)
                t = pool.do(lambda e: e.tensor_tensor(mr, mr, mz[0], ALU.subtract), t)
                t = pool.do(lambda e: e.tensor_copy(mz[1], mr), t)
                return pool.do(lambda e: e.tensor_tensor(mz[2], mr, mz[1], ALU.subtract), t)

            hs = n if now["main"] else 1
            yield from gather(0, hs)
            for _ in range(3):
                yield "wait"
            t_q = arrange(0, hs)
            if hs < n:
                for _ in gather(hs, n):
                    pass
            for _ in range((8 if now["main"] else 0)):
                yield

            pend = []
            def flush(lim, h):
                while len(pend) > lim:
                    j, tile, te = pend.pop(0)
                    first, last = tile == 0, tile == 2 * 16 - 1
                    pe.quiet(lambda e, j=j, tile=tile, first=first: e.matmul(
                        PV[0:2 * DH + 1, 0:U], VS[:, tile, h, :], EH[j], start=first, stop=False),
                        te, *(st["pv"] if first else ()), *t_vs[b])
                    spent[0] += 2 * U / 2400.0
                    tp = pe.do(lambda e, j=j, tile=tile, last=last: e.matmul(
                        PV[0:2 * DH + 1, 0:U], VS[:, tile, h, :], EL[j], start=False, stop=last))
                    st["e"][j] = tp
                    st["pvt"] = tp

            def load_ka(h):
                hr = slice(16 * h, 16 * h + 16)
                load_stack(l_a, [(KA[16 * r:16 * r + 16, :], KTC[b, m, hr, :]) for r, m in enumerate(KORD)],
                           (st["ka"], t_const) + ready[b, h // 8])

            for hl in range(n):
                h = h0 + hl
                i = h % 2
                load_ka(h)
                if hl == 1 and hs < n:
                    t_q = arrange(hs, n)
                trs = [(lambda s, a=a, w=w: s.bitcast(BF16)[:, a:a + w], QST[0:w, 3 * hl + c, :],
                        identb[0:w, 0:w]) for c, (a, w) in enumerate(CH[:2])]
                trs.append((lambda s: s.bitcast(BF16)[:, 256:256 + CH[2][1] + 1], QST[0:52, 3 * hl + 2, :],
                            identb[0:52, 0:52]))
                s, slot, tp = turn(C, trs, t_q, t_id)
                st["qst"] = tp
                t2 = C.free[s] = act.do(lambda e, slot=slot, i=i: e.copy(QT[i][:, 0:U], slot.bitcast(BF16)[:, 0:U]),
                                        tp, st["qt"][i])
                ld = l_a.all
                for _ in range(4):
                    yield
                for kc in range(NT):
                    s, slot, tp = fill(B, [(lambda s: s[:, 0:U], KA[0:99, 128 * kc:128 * kc + 128],
                                            QT[i][0:99, 0:U], True, True)], t2, ld)
                    j = st["ne"] % NE
                    st["ne"] += 1
                    te = B.free[s] = act.do(lambda e, slot=slot, j=j: e.activation(
                        E[j][:], slot[:, 0:U], ACT.Exp, scale=2 * SCALE / WS), tp, st["e"][j])
                    te = (pool if now["main"] or (j % 3 == 0 and not (hs < n and hl == 0)) else dve).do(lambda e, j=j: e.tensor_tensor(
                        EL[j], E[j][:], EH[j], ALU.subtract), te, st["e"][j])
                    pend.append((j, kc, te))
                    flush(PVLAG, h)
                    yield
                st["ka"] = st["qt"][i] = tp
                while pend:
                    flush(max(0, len(pend) - (2 if now["main"] else 8)), h)
                    yield
                t = act.do(lambda e, i=i: e.copy(OT[i][:, 0:U], PV[0:2 * DH + 1, 0:U]), st["pvt"],
                           st["ot"][i], t_const)
                st["pv"] = (t,)
                for _ in range(2):
                    yield
                trs = [(lambda s, c=c: s[:, 64 * c:64 * c + 2 * DH + 1], OT[i][:, 128 * c:128 * c + 128],
                        ident[0:2 * DH + 1, 0:2 * DH + 1]) for c in range(3)]
                s, slot, tp = turn(B, trs, t)
                st["ot"][i] = tp
                sv = slot[:, 0:192].rearrange("p (c d) -> p c d", c=3)
                t1 = dve.do(lambda e, sv=sv: e.reciprocal(rec[:], sv[:, :, 2 * DH]), tp, st.get("rec"))
                t = dve.do(lambda e, sv=sv: e.tensor_copy(osum[:], sv[:, :, 0:DH]), st.get("rec"))
                t = dve.do(lambda e, sv=sv: e.tensor_tensor(osum[:], osum[:], sv[:, :, DH:2 * DH], ALU.add), t)
                B.free[s] = t
                t = dve.do(lambda e, i=i: e.tensor_tensor(
                    OG[i][:], osum[:], rec[:].unsqueeze(2).broadcast_to([128, 3, DH]), ALU.mult),
                    t, t1, l_o[i].all)
                st["rec"] = t
                bv3 = bvb[:, DH * h:DH * h + DH].unsqueeze(1).broadcast_to([128, 3, DH])
                t = pool.do(lambda e, i=i, bv3=bv3: e.tensor_tensor(OG[i][:], OG[i][:], bv3, ALU.add), t, t_w)
                for c, (_, w) in enumerate(CH):
                    l_o[i].dma(pool, lambda e, i=i, c=c, w=w, k=3 * hl + c: e.indirect_dma_start(
                        out=AOr[b], out_offset=bass.IndirectOffsetOnAxis(ap=ixf[0:w, k:k + 1], axis=0),
                        in_=OG[i][0:w, c, :], in_offset=None), t, l_z.all)
                yield
            st["scat"] = (l_o[0].all, l_o[1].all)
            vs_free[0] = st["pvt"]
            st["lent"] = True
            B.slots.insert(1, PV[:])
            B.free.insert(1, st["pv"])

        l_f = [line(f"l_f{i}") for i in range(3)]
        l_out = [line(f"l_out{i}") for i in range(4)]
        def feed(b, scat):
            xb = x[b]
            edge = here()
            for e in (act, dve, pool, sp):
                e.waits(edge)
            pool.do(lambda e: e.memset(x1T[0][:, :, 0:1], 0.0))
            T = {}
            late = {}

            def g(*keys):
                return tuple(T.get(k) for k in keys)

            def rstd(t, q, tail):
                v, r = fmv[:, q, :], frs[:, q, :]
                t = pool.do(lambda e: e.tensor_scalar(r[:, 0:1], v[:, 1:2], EPS, None, ALU.add), t, *g(("n", q)))
                t = pool.do(lambda e: e.tensor_tensor(r[:, 0:1], r[:, 0:1], halfc[:], ALU.pow), t)
                if not tail:
                    t = pool.do(lambda e: e.tensor_tensor(r[:, 1:2], v[:, 0:1], r[:, 0:1], ALU.mult), t)
                    t = pool.do(lambda e: e.tensor_scalar(r[:, 1:2], r[:, 1:2], -1.0, 0.0, ALU.mult, ALU.add), t)
                return t

            def norm(src, dst, q, tail, *toks):
                v, r = fmv[:, q, :], frs[:, q, :]
                if tail:
                    t = dve.do(lambda e: e.tensor_scalar(dst, src, v[:, 0:1], r[:, 0:1], ALU.subtract, ALU.mult), *toks)
                else:
                    t = pool.do(lambda e: e.tensor_scalar(dst, src, r[:, 0:1], r[:, 1:2], ALU.mult, ALU.add), *toks)
                T["n", q] = t
                return t

            def stats(src, q, *toks):
                i = q % 2
                t = dve.do(lambda e: e.bn_stats(fst[:, i, :], src), *toks, *g(("st", i)))
                t = T["st", i] = dve.do(lambda e: e.bn_aggr(fmv[:, q, :], fst[:, i, :]), t, *g(("n", q)))
                return t

            def f0(t):
                i = t % 3
                late[t] = not now["main"]
                l_f[i].dma(sp, lambda e: e.dma_start(fx[i], xb[128 * t:128 * t + 128, :]),
                           *scat, *g(("y", t - 3), ("T0", t - 3), ("xb", t - 3)))
                T["ld", t] = l_f[i].dma(sp, lambda e: e.dma_start(fao[i], AO[b][128 * t:128 * t + 128, :]))

            def f1(t):
                i, j = t % 3, t % 2
                s, slot, tp = turn(B, [(lambda s, k=k: s[:, 128 * k:128 * k + 128],
                                        fao[i][:, 128 * k:128 * k + 128], ident[:]) for k in range(2)], *g(("ld", t)))
                T["T0", t] = tp
                T["aT", t] = B.free[s] = act.do(lambda e: e.copy(
                    faT[j].rearrange("p k n -> p (k n)"), slot[:, 0:256]), tp, *g(("yp", t - 2)))
                T["xb", t] = pool.do(lambda e: e.tensor_tensor(fx[i], fx[i], bob[:], ALU.add), *g(("ld", t)), t_w)

            def f2(t):
                i, j = t % 3, t % 2
                s, slot, tp = yield from fill_slowly(B, [(lambda s: s[:, 0:D], faT[j][:, k, :], W2["o"][:, k, :], k == 0, k == 1)
                                        for k in range(2)], t_w, *g(("aT", t)))
                T["yp", t] = tp
                t1 = T["y", t] = B.free[s] = dve.do(lambda e: e.tensor_tensor(
                    fh[j], slot[:, 0:D], fx[i], ALU.add), tp, *g(("xb", t), ("x1", t - 2)))
                T["s1", t] = rstd(stats(fh[j], j, t1), j, late[t])

            def f3(t):
                j = t % 2
                T["x1", t] = norm(fh[j], fx1[t % 4], j, late[t], *g(("s1", t), ("o2", t - 4), ("T1", t - 4)))

            def f4(t):
                i = t % 3
                s, slot, tp = turn(B, [(lambda s, k=k: s[:, 128 * k:128 * k + 128],
                                        fx1[t % 4][:, 128 * k:128 * k + 128], ident[:]) for k in range(2)],
                                   *g(("x1", t)))
                T["T1", t] = tp
                sv = slot[:, 0:256].rearrange("p (k n) -> p k n", k=2)
                ta = act.do(lambda e: e.copy(x1T[i][:, :, 1:129], sv), tp, *g(("mx", t - 3), ("mx", t - 2)))
                T["x1T", t] = B.free[s] = act.do(lambda e: e.copy(x1T[(t + 1) % 3][:, :, 0:1], sv[:, :, 127:128]))
                if late[t]:
                    for m, cb in enumerate((MR1, MK1)):
                        for k in range(2):
                            T["fmp", t] = act.do(lambda e, m=m, k=k, cb=cb: e.mul(
                                fmp[m][:, k, :], x1T[i][:, k, 0:128], cols[:, cb.start + k:cb.start + k + 1]),
                                ta, t_cols, *g(("mx", t - 1)))

            def f5(t):
                i, j = t % 3, t % 2
                cur, prv = x1T[i][:, :, 1:129], x1T[i][:, :, 0:128]
                for m, (ca, cb) in enumerate(((MR, MR1), (MK, MK1))):
                    fm = (fm0, fm1)[m][j]
                    w = g(("x1T", t), ("fmp", t), ("mx", t - 1), ("r", t - 2), ("k", t - 2))
                    for k in range(2):
                        if late[t]:
                            T["mx", t] = dve.do(lambda e, m=m, k=k, ca=ca, fm=fm: e.scalar_tensor_tensor(
                                out=fm[:, k, :], in0=cur[:, k, :], scalar=cols[:, ca.start + k:ca.start + k + 1],
                                in1=fmp[m][:, k, :], op0=ALU.mult, op1=ALU.add), *w)
                        else:
                            pool.do(lambda e, m=m, k=k, cb=cb: e.tensor_scalar(
                                fmp[m][:, k, :], prv[:, k, :], cols[:, cb.start + k:cb.start + k + 1], 0.0,
                                ALU.mult, ALU.add), *w, t_cols)
                            tq = pool.do(lambda e, k=k, ca=ca, fm=fm: e.tensor_scalar(
                                fm[:, k, :], cur[:, k, :], cols[:, ca.start + k:ca.start + k + 1], 0.0, ALU.mult,
                                ALU.add))
                    if not late[t]:
                        T["mx", t] = pool.do(lambda e, m=m, fm=fm: e.tensor_tensor(fm, fm, fmp[m], ALU.add), tq)

            def f6(t):
                j = t % 2
                s, slot, tp = yield from fill_slowly(B, [(lambda s: s[:, 0:D], fm0[j][:, k, :], W2["rT"][:, k, :], k == 0, k == 1)
                                       for k in range(2)], t_ffw, *g(("mx", t)))
                T["r", t] = tp
                T["th", t] = B.free[s] = act.do(lambda e: e.activation(fr[j], slot[:, 0:D], ACT.Tanh, scale=0.5),
                                                tp, *g(("o1", t - 2)))
                yield
                s2, slot2, tp = yield from fill_slowly(B, [(lambda s, m=m: s[:, 128 * m:128 * m + 128],
                                          W2["kT"][:, k, 128 * m:128 * m + 128], fm1[j][:, k, :], k == 0, k == 1)
                                         for m in range(2) for k in range(2)])
                T["k", t] = tp
                tk = B.free[s2] = act.do(lambda e: e.activation(
                    fk[j].rearrange("p k n -> p (k n)"), slot2[:, 0:256], ACT.Relu), tp, *g(("sq", t - 2)))
                if late[t]:
                    T["sq", t] = act.do(lambda e: e.activation(fk2[j], fk[j], ACT.Square), tk, *g(("v", t - 2)))
                else:
                    T["sq", t] = pool.do(lambda e: e.tensor_tensor(fk2[j], fk[j], fk[j], ALU.mult), tk,
                                         *g(("v", t - 2)))

            def f7(t):
                i, j = t % 4, t % 2
                s, slot, tp = yield from fill_slowly(B, [(lambda s: s[:, 0:D], fk2[j][:, k, :], W2["vT"][:, k, :], k == 0, k == 1)
                                        for k in range(2)], *g(("sq", t)))
                T["v", t] = tp
                t1 = T["o1", t] = B.free[s] = dve.do(lambda e: e.scalar_tensor_tensor(
                    out=fo[i], in0=fr[j], scalar=1.0, in1=slot[:, 0:D], op0=ALU.add, op1=ALU.mult),
                    tp, l_out[i].all, *g(("th", t), ("o3", t - 4)))
                T["o2", t] = (dve if late[t] else pool).do(lambda e: e.tensor_tensor(
                    fo[i], fo[i], fx1[t % 4], ALU.add), t1)

            def f8(t):
                i, j = t % 4, t % 2
                T["s2", t] = rstd(stats(fo[i], 2 + j, *g(("o2", t))), 2 + j, late[t])

            def f9(t):
                i, j = t % 4, t % 2
                tn = T["o3", t] = norm(fo[i], fo[i], 2 + j, late[t], *g(("s2", t)))
                l_out[i].dma(sp, lambda e: e.dma_start(out[b, 128 * t:128 * t + 128, :], fo[i]), tn)

            stages = [f0, f1, f2, f3, f4, f5, f6, f7, f8, f9]
            for k in range(NT + len(stages) - 1):
                for n, f in reversed(list(enumerate(stages))):
                    if 0 <= k - n < NT:
                        yield from f(k - n) or ()
                        if n in (8, 7, 6, 4, 2, 0):
                            yield

        lanes = {"s": [], "a": [], "b": []}

        def step(lane):
            q = lanes[lane]
            while q:
                try:
                    return next(q[0]) or "work"
                except StopIteration:
                    q.pop(0)
            return None

        def until(key):
            while key not in ready:
                assert step("b")

        done = {}

        def select_job(g):
            while (1, 1) not in ready:
                yield "wait"
            yield from select(g, t_cap[g])

        def attend_job(g):
            while g not in sel or st["open"]:
                yield "wait"
            yield from attend(g)
            done[g] = st["scat"]

        def rest():
            while G1 - 1 not in done:
                yield "wait"
            yield from values(1)
            done["v"] = True
            yield from feed(0, done[G1 - 1])

        def wait_values():
            while "v" not in done:
                yield "wait"

        t_cap = {}
        lanes["b"] += [project(0)]
        until((0, 0))
        now["fast"] = False
        lanes["b"] += [values(0), project(1), rest()]
        load_head(0)
        n = 0
        credit = 0.0

        def background():
            step("s")
            s0 = spent[0]
            for lane in ("a", "b"):
                if spent[0] - s0 < credit and (lane == "a" or st["lent"] or st["open"]):
                    step(lane)
            return spent[0] - s0

        for g, (b, h0, cnt) in enumerate(GROUPS):
            for hl in range(cnt):
                if n + 1 < NB * H:
                    until(((n + 1) // H, (n + 1) % H // 8))
                    load_head(n + 1)
                for t in range(NT):
                    for u in range(2):
                        td = period(n, g, hl, t, u)
                        credit = min(credit + BUDGET, 4 * BUDGET)
                        credit -= background()
                n += 1
            t_cap[g] = capture(g, td)
            lanes["s"].append(select_job(g))
            if g == G1:
                lanes["a"].append(wait_values())
            lanes["a"].append(attend_job(g))
        for ring, m in ((C, 0), (B, 1)):
            ring.slots += [DP[:, m, 0:512], DP[:, m, 512:1024]]
            ring.free += [DR.free[m]] * 2
        now["main"] = False
        more = True
        while more:
            more = selecting = step("s") is not None
            for lane in ("a", "b") if selecting else ("a", "b", "a", "b"):
                more = step(lane) is not None or more
        B.slots += C.slots
        B.free += C.free
        for _ in feed(1, st["scat"]):
            pass
        for ln in (l_w, l_z, l_m, l_i, l_g, *l_s, *l_q, l_a, *l_o, *l_f, *l_out):
            sp.waits([ln.all])

        ctx.enter_context(nc.allow_non_contiguous_dma(reason="columns, indices and maxima are small"))
        block = ctx.enter_context(nc.Block())
        block.tensor(pe.run)
        block.scalar(act.run)
        block.vector(dve.run)
        block.gpsimd(pool.run)
        block.sync(sp.run)


_INS = ['L0_attn_x', 'L0_attn_Wq', 'L0_attn_bq', 'L0_attn_Wk', 'L0_attn_bk', 'L0_attn_Wv', 'L0_attn_bv',
        'L0_attn_Wo', 'L0_attn_bo', 'L0_ffn_W_r', 'L0_ffn_W_k', 'L0_ffn_W_v', 'L0_ffn_mu_r', 'L0_ffn_mu_k']


def kernel(**inputs):
    import numpy as np
    import concourse.bacc as bacc
    from concourse.bass_utils import run_bass_kernel_spmd as run

    nc = bacc.Bacc("TRN2", target_bir_lowering=False, num_devices=1)
    arrays, args = {}, []
    for name in _INS:
        a = np.ascontiguousarray(inputs[name])
        arrays[f"in_{name}"] = a
        args.append(nc.dram_tensor(f"in_{name}", a.shape, F32, kind="ExternalInput").ap())
    out = nc.dram_tensor("out_0", (NB, L, D), F32, kind="ExternalOutput").ap()
    attention_rwkv(nc, *args, out)
    r = run(nc, [arrays], core_ids=[0])
    return r.results[0]["out_0"]
```
